# Optimizing a Trainium2 kernel written in Bass

```python
import numpy as np
import jax
import jax.numpy as jnp

def _softmax(x, axis=-1):
    return jax.nn.softmax(x, axis=axis)

def _gelu(x):
    return jax.nn.gelu(x, approximate=True)

def _silu(x):
    return jax.nn.silu(x)

def _sigmoid(x):
    return jax.nn.sigmoid(x)

def _layernorm(x, axis=-1, eps=1e-05):
    m = jnp.mean(x, axis=axis, keepdims=True)
    v = jnp.var(x, axis=axis, keepdims=True)
    return (x - m) / jnp.sqrt(v + eps)

def _scatter_add(tgt, idx, src, axis=0):
    return tgt.at[idx].add(src)

def _segment_sum(src, seg, n):
    return jax.ops.segment_sum(src, seg, n)
kernel_name = 'mk_decoder_preln_d1_seqx_r4_451276'

def setup_inputs(seed: int=0):
    np.random.seed(seed)
    _w = jnp.asarray

    def _rec_inputs():
        import jax
        import jax.numpy as jnp
        _rk = jax.random.key(seed)
        x = 7.22e-05 + 1 * jax.random.normal(jax.random.fold_in(_rk, 1), (1, 2048, 256), jnp.float32)
        _lenS = 2048 - jax.random.randint(jax.random.fold_in(_rk, 7), (1,), 0, max(1, 2048 // 4) + 1, jnp.int32)
        _lenS2 = 1601 - jax.random.randint(jax.random.fold_in(_rk, 8), (1,), 0, max(1, 1601 // 4) + 1, jnp.int32)
        _ctx_1024P = jax.random.normal(jax.random.fold_in(_rk, 11), (1, 16, 256), jnp.float32)
        _ctx_1024c = jax.random.dirichlet(jax.random.fold_in(_rk, 511), 0.3 * jnp.ones((16,), jnp.float32), (1, 1601))
        _ctx_1024t = jnp.einsum('bsk,bkd->bsd', _ctx_1024c, _ctx_1024P)
        _ctx_1024t = _ctx_1024t * jax.lax.rsqrt(jnp.mean(jnp.square(_ctx_1024t)) + 1e-12) * 0.953939
        ctx_1024 = 4.13588e-05 + 0.999923 * (_ctx_1024t + 0.3 * jax.random.normal(jax.random.fold_in(_rk, 611), (1, 1601, 256), jnp.float32))
        _validS = jnp.arange(2048)[None, :] < _lenS[:, None]
        _validS2 = jnp.arange(1601)[None, :] < _lenS2[:, None]
        _causal = jnp.tril(jnp.ones((2048, 2048), dtype=bool))
        mask_BxSxS2_ik1 = jnp.where(jnp.broadcast_to(_validS2[:, None, :], (1, 2048, 1601)), 1, 0).astype(jnp.int32)
        return (x, ctx_1024, mask_BxSxS2_ik1)
    x, ctx_1024, mask_BxSxS2_ik1 = _rec_inputs()

    def _L0_attn_setup():
        import jax, jax.numpy as jnp
        import numpy as np
        N_HEAD = 16
        PAGE_SIZE = 64
        ROPE_THETA = 10000.0

        def _rope_tables(T, D, dtype):
            inv = 1.0 / ROPE_THETA ** (np.arange(0, D, 2, dtype=np.float32) / D)
            ang = np.outer(np.arange(T, dtype=np.float32), inv)
            return (jnp.asarray(np.cos(ang), dtype), jnp.asarray(np.sin(ang), dtype))

        def _apply_rope(x, cos, sin):
            x1 = x[..., 0::2]
            x2 = x[..., 1::2]
            c = cos[None, :, None, :]
            s = sin[None, :, None, :]
            out = jnp.stack([x1 * c - x2 * s, x1 * s + x2 * c], axis=-1)
            return out.reshape(x.shape)
        key = jax.random.key(seed)
        ks = jax.random.split(key, 6)
        B, T, E = (2, 512, 256)
        L = E // 2
        sc = lambda fan: 1.0 / np.sqrt(fan)
        return {'x': jax.random.normal(ks[0], (B, T, E), jnp.float32), 'wq': jax.random.normal(ks[1], (E, E), jnp.float32) * sc(E), 'w_down': jax.random.normal(ks[2], (E, L), jnp.float32) * sc(E), 'wk_up': jax.random.normal(ks[3], (L, E), jnp.float32) * sc(L), 'wv_up': jax.random.normal(ks[4], (L, E), jnp.float32) * sc(L), 'wo': jax.random.normal(ks[5], (E, E), jnp.float32) * sc(E)}
    _L0_attn_all = _L0_attn_setup()
    _L0_attn_in = {k: v for k, v in _L0_attn_all.items() if k in ('wq', 'w_down', 'wk_up', 'wv_up', 'wo')}
    del _L0_attn_all

    def _L0_xattn_setup():
        import jax, jax.numpy as jnp
        import numpy as np
        B, S, D_IN = (4, 512, 256)
        N_HEAD, D_ATTN, D_OUT = (16, 64, 256)
        D_H = N_HEAD * D_ATTN
        key = jax.random.key(seed)
        ks = jax.random.split(key, 12)
        s = 1.0 / np.sqrt(D_IN)
        inp = {'q': jax.random.normal(ks[0], (B, S, D_IN), dtype=jnp.float32), 'k': jax.random.normal(ks[1], (B, S, D_IN), dtype=jnp.float32), 'v': jax.random.normal(ks[2], (B, S, D_IN), dtype=jnp.float32), 'mask': jax.random.randint(ks[3], (B, S, S), 0, 2, dtype=jnp.int32), 'Wq': jax.random.normal(ks[4], (D_H, D_IN), dtype=jnp.float32) * s, 'bq': jnp.zeros((D_H,), dtype=jnp.float32), 'Wk': jax.random.normal(ks[5], (D_H, D_IN), dtype=jnp.float32) * s, 'bk': jnp.zeros((D_H,), dtype=jnp.float32), 'Wv': jax.random.normal(ks[6], (D_H, D_IN), dtype=jnp.float32) * s, 'bv': jnp.zeros((D_H,), dtype=jnp.float32), 'Wo': jax.random.normal(ks[7], (D_OUT, D_H), dtype=jnp.float32) * (1.0 / np.sqrt(D_H)), 'bo': jnp.zeros((D_OUT,), dtype=jnp.float32)}
        return inp
    _L0_xattn_all = _L0_xattn_setup()
    _L0_xattn_in = {k: v for k, v in _L0_xattn_all.items() if k in ('Wq', 'bq', 'Wk', 'bk', 'Wv', 'bv', 'Wo', 'bo')}
    del _L0_xattn_all

    def _L0_ffn_setup():
        import jax, jax.numpy as jnp
        import numpy as np
        LN_EPS = 0.001
        EPS = 1e-05
        QB = 128.0

        def ste_round(x):
            return x + jax.lax.stop_gradient(jnp.round(x) - x)
        key = jax.random.key(seed)
        k1, k2 = jax.random.split(key)
        x = jax.random.normal(k1, (4, 2048, 256), dtype=jnp.float32)
        weight = jax.random.normal(k2, (256, 256), dtype=jnp.float32) * 0.02
        ln_gamma = jnp.ones((256,), dtype=jnp.float32)
        ln_beta = jnp.zeros((256,), dtype=jnp.float32)
        return {'x': x, 'weight': weight, 'ln_gamma': ln_gamma, 'ln_beta': ln_beta}
    _L0_ffn_all = _L0_ffn_setup()
    _L0_ffn_in = {k: v for k, v in _L0_ffn_all.items() if k in ('weight', 'ln_gamma', 'ln_beta')}
    del _L0_ffn_all
    return {'x': x, 'ctx_1024': ctx_1024, 'mask_BxSxS2_ik1': mask_BxSxS2_ik1, 'L0_attn_wq': _L0_attn_in['wq'], 'L0_attn_w_down': _L0_attn_in['w_down'], 'L0_attn_wk_up': _L0_attn_in['wk_up'], 'L0_attn_wv_up': _L0_attn_in['wv_up'], 'L0_attn_wo': _L0_attn_in['wo'], 'L0_xattn_Wq': _L0_xattn_in['Wq'], 'L0_xattn_bq': _L0_xattn_in['bq'], 'L0_xattn_Wk': _L0_xattn_in['Wk'], 'L0_xattn_bk': _L0_xattn_in['bk'], 'L0_xattn_Wv': _L0_xattn_in['Wv'], 'L0_xattn_bv': _L0_xattn_in['bv'], 'L0_xattn_Wo': _L0_xattn_in['Wo'], 'L0_xattn_bo': _L0_xattn_in['bo'], 'L0_ffn_weight': _L0_ffn_in['weight'], 'L0_ffn_ln_gamma': _L0_ffn_in['ln_gamma'], 'L0_ffn_ln_beta': _L0_ffn_in['ln_beta']}

def reference(x, ctx_1024, mask_BxSxS2_ik1, L0_attn_wq, L0_attn_w_down, L0_attn_wk_up, L0_attn_wv_up, L0_attn_wo, L0_xattn_Wq, L0_xattn_bq, L0_xattn_Wk, L0_xattn_bk, L0_xattn_Wv, L0_xattn_bv, L0_xattn_Wo, L0_xattn_bo, L0_ffn_weight, L0_ffn_ln_gamma, L0_ffn_ln_beta):
    import jax
    import jax.numpy as jnp

    def _L0_attn_ref(x, wq, w_down, wk_up, wv_up, wo):
        import jax, jax.numpy as jnp
        import numpy as np
        N_HEAD = 16
        PAGE_SIZE = 64
        ROPE_THETA = 10000.0

        def _rope_tables(T, D, dtype):
            inv = 1.0 / ROPE_THETA ** (np.arange(0, D, 2, dtype=np.float32) / D)
            ang = np.outer(np.arange(T, dtype=np.float32), inv)
            return (jnp.asarray(np.cos(ang), dtype), jnp.asarray(np.sin(ang), dtype))

        def _apply_rope(x, cos, sin):
            x1 = x[..., 0::2]
            x2 = x[..., 1::2]
            c = cos[None, :, None, :]
            s = sin[None, :, None, :]
            out = jnp.stack([x1 * c - x2 * s, x1 * s + x2 * c], axis=-1)
            return out.reshape(x.shape)
        B, T, E = x.shape
        H = N_HEAD
        D = E // H
        q = (x @ wq).reshape(B, T, H, D)
        lat = x @ w_down
        k = (lat @ wk_up).reshape(B, T, H, D)
        v = (lat @ wv_up).reshape(B, T, H, D)
        cos, sin = _rope_tables(T, D, x.dtype)
        q = _apply_rope(q, cos, sin)
        k = _apply_rope(k, cos, sin)
        scale = 1.0 / jnp.sqrt(jnp.asarray(D, x.dtype))
        scores = jnp.einsum('bqhd,bkhd->bhqk', q, k) * scale
        pages = jnp.arange(T) // PAGE_SIZE
        allowed = pages[None, :] <= pages[:, None]
        scores = jnp.where(allowed[None, None], scores, jnp.finfo(scores.dtype).min)
        attn = jax.nn.softmax(scores, axis=-1)
        out = jnp.einsum('bhqk,bkhd->bqhd', attn, v).reshape(B, T, E)
        return out @ wo

    def _L0_xattn_ref(q, k, v, mask, Wq, bq, Wk, bk, Wv, bv, Wo, bo):
        import jax, jax.numpy as jnp
        import numpy as np
        B, S, D_IN = (4, 512, 256)
        N_HEAD, D_ATTN, D_OUT = (16, 64, 256)
        D_H = N_HEAD * D_ATTN
        Q = q @ Wq.T + bq
        K = k @ Wk.T + bk
        V = v @ Wv.T + bv
        d_k = Q.shape[-1]
        e = jnp.einsum('bsd,btd->bst', Q, K) / jnp.sqrt(jnp.float32(d_k))
        MASK_FILL = jnp.float32(-2 ** 15)
        e = jnp.where(mask == 0, MASK_FILL, e)
        a = jax.nn.softmax(e, axis=-1)
        y = jnp.einsum('bst,btd->bsd', a, V)
        return y @ Wo.T + bo

    def _L0_ffn_ref(x, weight, ln_gamma, ln_beta):
        import jax, jax.numpy as jnp
        import numpy as np
        LN_EPS = 0.001
        EPS = 1e-05
        QB = 128.0

        def ste_round(x):
            return x + jax.lax.stop_gradient(jnp.round(x) - x)
        mu = jnp.mean(x, axis=-1, keepdims=True)
        var = jnp.var(x, axis=-1, keepdims=True)
        xn = (x - mu) * jax.lax.rsqrt(var + LN_EPS) * ln_gamma + ln_beta
        beta = jnp.mean(jnp.abs(weight))
        w_q = jnp.clip(ste_round(weight / (beta + EPS)), -1.0, 1.0)
        gamma = jnp.max(jnp.abs(xn))
        xq = jnp.clip(xn * QB / gamma, -QB + EPS, QB - EPS)
        y = jnp.einsum('bsd,du->bsu', xq, w_q)
        return y * (gamma * beta / QB)
    x = x + _L0_attn_ref(_layernorm(x, axis=-1), L0_attn_wq, L0_attn_w_down, L0_attn_wk_up, L0_attn_wv_up, L0_attn_wo)
    x = x + _L0_xattn_ref(_layernorm(x, axis=-1), ctx_1024, ctx_1024, mask_BxSxS2_ik1, L0_xattn_Wq, L0_xattn_bq, L0_xattn_Wk, L0_xattn_bk, L0_xattn_Wv, L0_xattn_bv, L0_xattn_Wo, L0_xattn_bo)
    x = x + _L0_ffn_ref(_layernorm(x, axis=-1), L0_ffn_weight, L0_ffn_ln_gamma, L0_ffn_ln_beta)
    return x

_drawn_inputs = setup_inputs


def setup_inputs(seed=0):
    import zlib

    import numpy as np

    out = dict(_drawn_inputs(seed))
    spreads = {'L0_xattn_bq': (0.0, 0.377),
     'L0_xattn_bk': (0.0, 0.8),
     'L0_xattn_bv': (0.0, 0.1),
     'L0_xattn_bo': (0.0, 0.1),
     'L0_ffn_ln_gamma': (1.0, 0.2),
     'L0_ffn_ln_beta': (0.0, 0.458)}
    factors = {}
    for name, (base, spread) in spreads.items():
        noise = np.random.default_rng([zlib.crc32(name.encode()), seed]).standard_normal(out[name].shape)
        drawn = base * np.exp(spread * noise) if base else spread * noise
        out[name] = jnp.asarray(drawn.astype(out[name].dtype))
    for name, factor in factors.items():
        out[name] = (out[name] * factor).astype(out[name].dtype)
    return out
```

```python
from contextlib import ExitStack

import concourse.bass as bass
from concourse import mybir

F32 = mybir.dt.float32
BF16 = mybir.dt.bfloat16
I32 = mybir.dt.int32
U32 = mybir.dt.uint32
ALU = mybir.AluOpType
ACT = mybir.ActivationFunctionType
AX_X = mybir.AxisListType.X
ReduceOp = bass.bass_isa.ReduceOp

P = 128
T, E = 2048, 256
EC = E // P
H, D = 16, 16
HALF = D // 2
TILES = T // P
BLK = 512
NB = T // BLK
TPB = BLK // P
PAGE = 64
G = 4
NG = H // G
VW = D + 1
LN_EPS = 1e-5
ATTN_SCALE = float(D) ** -0.5
NEG_BIG = -1e30

Q_PIECES = [0, 0, 0, 1, 1, 2]
K_PIECES = [0, 1, 2, 0, 1, 0]
TERM_ROWS = D * len(Q_PIECES)
SHIFT_ROWS = 2
STACK = TERM_ROWS + SHIFT_ROWS

S2 = 1601
S2_TILES = -(-S2 // P)
S2_TAIL = S2 - (S2_TILES - 1) * P
DH = 1024
HC = DH // P
X_SCALE = float(DH) ** -0.5
X_FILL = -(2.0 ** 15) / X_SCALE

QB, FFN_EPS, FFN_LN_EPS = 128.0, 1e-5, 1e-3

def banks(psum, first, n=1):
    return psum[:, first * BLK:(first + n) * BLK]

def project(nc, ctx, io, keep, psum):
    def sb(name, shape, dt=F32):
        return ctx.enter_context(nc.sbuf_tensor(name, shape, dt))

    def sem(name):
        return ctx.enter_context(nc.semaphore(name))

    x, ident, v_all = keep["x"], keep["ident"], keep["v_all"]
    w_q = sb("w_q", [P, EC, E])
    w_lat = sb("w_lat", [P, EC, P])
    w_k = sb("w_k", [P, E])
    w_v = sb("w_v", [P, E])
    cos = sb("cos", [P, NB, BLK])
    sin = sb("sin", [P, NB, BLK])
    stats = sb("stats", [P, TPB, 6])
    mv = sb("mv", [P, TPB, 2])
    var = sb("var", [P, TPB])
    rstd = sb("rstd", [P, TPB])
    minus_half = sb("minus_half", [P, TPB])
    eps = sb("eps", [P, TPB])
    xn = sb("xn", [P, TPB, E])
    xn_t = sb("xn_t", [P, EC, BLK])
    lat_t = sb("lat_t", [P, BLK])
    prod_a = sb("prod_a", [P, 4, BLK])
    prod_b = sb("prod_b", [P, 4, BLK])
    rot = sb("rot", [P, 4, BLK])
    rest = sb("rest", [P, 4, BLK])
    piece = [sb(f"piece{n}", [P, 4, BLK], BF16) for n in range(3)]

    x_bank = [banks(psum, 0), banks(psum, 1)]
    lat_bank = banks(psum, 2)
    v_bank = [banks(psum, 2), banks(psum, 3)]
    qk_bank = [[banks(psum, 4), banks(psum, 5)], [banks(psum, 6), banks(psum, 7)]]

    x_loaded = sem("x_loaded")
    w_loaded = sem("w_loaded")
    rope_loaded = sem("rope_loaded")
    ident_ready = sem("ident_ready")
    const_ready = sem("const_ready")
    stats_done = sem("stats_done")
    waits_met = sem("waits_met")
    mv_done = sem("mv_done")
    var_done = sem("var_done")
    rstd_done = sem("rstd_done")
    xn_ready = sem("xn_ready")
    xt_ready = sem("xt_ready")
    xt_copied = sem("xt_copied")
    lat_ready = sem("lat_ready")
    lat_copied = sem("lat_copied")
    v_ready = sem("v_ready")
    v_copied = sem("v_copied")
    qk_ready = sem("qk_ready")
    prod_done = sem("prod_done")
    rot_done = sem("rot_done")
    rest_done = sem("rest_done")
    piece_done = [sem(f"piece_done{n}") for n in range(3)]
    piece_sent = [sem(f"piece_sent{n}") for n in range(3)]

    with nc.Block() as block:

        @block.sync
        def _(sp):
            sp.dma_start(x[:, :, :], io["x"].rearrange("(t p) e -> p t e", p=P)).then_inc(x_loaded, 16)
            sp.dma_start(w_q[:, :, :], io["wq"].rearrange("(c p) e -> p c e", p=P)).then_inc(w_loaded, 16)
            sp.dma_start(w_lat[:, :, :], io["w_down"].rearrange("(c p) e -> p c e", p=P)).then_inc(w_loaded, 16)
            sp.dma_start(w_k[:, :], io["wk_up"]).then_inc(w_loaded, 16)
            sp.dma_start(w_v[:, :], io["wv_up"]).then_inc(w_loaded, 16)
            with sp.Fori(0, NB) as tb:
                for n in range(3):
                    for u in range(4):
                        sp.wait_ge(piece_done[n], tb * 4 + u + 1)
                        dst = io["pieces"][u // 2, tb, n, u % 2].rearrange("f h t -> h f t")
                        sp.dma_start(dst, piece[n][:, u, :]).then_inc(piece_sent[n], 16)
            for n in range(3):
                sp.wait_ge(piece_sent[n], 16 * 4 * NB)

        @block.gpsimd
        def _(pool):
            nc.gpsimd.memset(ident[:, :], 0.0).then_inc(ident_ready, 1)
            nc.gpsimd.memset(minus_half[:, :], -0.5).then_inc(const_ready, 1)
            nc.gpsimd.memset(v_all[:, :, :, D:VW], 1.0).then_inc(const_ready, 1)
            nc.gpsimd.memset(keep["mask_row"][:, :], 0.0).then_inc(const_ready, 1)
            nc.gpsimd.memset(keep["ones"][:, :], 1.0).then_inc(const_ready, 1)
            pool.wait_ge(ident_ready, 1)
            nc.gpsimd.affine_select(out=ident[:, :], in_=ident[:, :], compare_op=ALU.not_equal, fill=1.0,
                                    base=0, pattern=[[-1, P]], channel_multiplier=1).then_inc(ident_ready, 1)
            nc.gpsimd.memset(eps[:, :], LN_EPS).then_inc(const_ready, 1)
            pool.wait_ge(const_ready, 5)
            nc.gpsimd.memset(keep["mask_row"][0:1, 0:PAGE], NEG_BIG).then_inc(const_ready, 1)

            def norm(tb):
                pool.wait_ge(mv_done, tb * TPB + TPB)
                nc.gpsimd.tensor_tensor(var[:, :], mv[:, :, 1], eps[:, :], ALU.add).then_inc(var_done, 1)
                pool.wait_ge(var_done, tb + 1)
                nc.gpsimd.tensor_tensor(rstd[:, :], var[:, :], minus_half[:, :], ALU.pow).then_inc(rstd_done, 1)

            def rotate(tb):
                for u in range(4):
                    pool.wait_ge(prod_done, tb * 8 + 2 * u + 2)
                    pool.wait_ge(piece_done[0], tb * 4)
                    pool.wait_ge(rest_done, tb * 4)
                    op = ALU.add if u % 2 else ALU.subtract
                    nc.gpsimd.tensor_tensor(rot[:, u, :], prod_a[:, u, :], prod_b[:, u, :], op).then_inc(rot_done, 1)
                pool.wait_ge(piece_sent[2], tb * 64)
                for u in range(4):
                    pool.wait_ge(rest_done, tb * 4 + u + 1)
                    pool.wait_ge(piece_done[1], tb * 4 + u + 1)
                    nc.gpsimd.tensor_tensor(piece[2][:, u, :], rest[:, u, :], piece[1][:, u, :],
                                            ALU.subtract).then_inc(piece_done[2], 1)

            pool.wait_ge(const_ready, 6)
            norm(0)
            with pool.Fori(0, NB - 1) as tb:
                norm(tb + 1)
                rotate(tb)
            rotate(NB - 1)

        @block.vector
        def _(dve):
            def norm(tb):
                for k in range(TPB):
                    nc.vector.bn_stats(out=stats[:, k, :], in_=x[:, tb * TPB + k, :]).then_inc(stats_done, 1)
                dve.wait_ge(stats_done, tb * TPB + TPB)
                dve.wait_ge(var_done, tb)
                dve.sem_inc(waits_met, 1)
                for k in range(TPB):
                    nc.vector.bn_aggr(out=mv[:, k, :], in_=stats[:, k, :]).then_inc(mv_done, 1)
                dve.wait_ge(rstd_done, tb + 1)
                dve.wait_ge(xt_ready, tb * EC)
                for k in range(TPB):
                    nc.vector.tensor_scalar(xn[:, k, :], x[:, tb * TPB + k, :], mv[:, k, 0:1], rstd[:, k:k + 1],
                                            ALU.subtract, ALU.mult).then_inc(xn_ready, 1)

            def rotate(tb):
                dve.wait_ge(rot_done, tb * 4)
                for s in range(2):
                    dve.wait_ge(qk_ready, tb * 2 + s + 1)
                    even, odd = qk_bank[s]
                    for u, a, b in ((2 * s, cos, sin), (2 * s + 1, sin, cos)):
                        nc.vector.tensor_tensor(prod_a[:, u, :], even, a[:, tb, :], ALU.mult).then_inc(prod_done, 1)
                        nc.vector.tensor_tensor(prod_b[:, u, :], odd, b[:, tb, :], ALU.mult).then_inc(prod_done, 1)
                dve.wait_ge(piece_done[2], tb * 4)
                for u in range(4):
                    dve.wait_ge(piece_done[0], tb * 4 + u + 1)
                    nc.vector.tensor_tensor(rest[:, u, :], rot[:, u, :], piece[0][:, u, :],
                                            ALU.subtract).then_inc(rest_done, 1)

            dve.wait_ge(x_loaded, 16)
            norm(0)
            dve.wait_ge(rope_loaded, 32)
            with dve.Fori(0, NB - 1) as tb:
                norm(tb + 1)
                rotate(tb)
            rotate(NB - 1)

        @block.scalar
        def _(act):
            for name, tile in (("cos", cos), ("sin", sin)):
                table = io[name].rearrange("f (b t) -> f (b t)", t=BLK)
                src = bass.AP(table.tensor, 0, [[0, H], [T, HALF], [1, T]])
                act.dma_start(tile[:, :, :].rearrange("p b t -> p (b t)"), src).then_inc(rope_loaded, 16)

            def project_copies(tb):
                act.wait_ge(qk_ready, tb * 2)
                for c in range(EC):
                    act.wait_ge(xt_ready, tb * EC + c + 1)
                    nc.scalar.activation(xn_t[:, c, :], x_bank[c], ACT.Copy).then_inc(xt_copied, 1)
                act.wait_ge(lat_ready, tb + 1)
                act.wait_ge(v_ready, tb * 2)
                nc.scalar.activation(lat_t[:, :], lat_bank, ACT.Copy).then_inc(lat_copied, 1)
                for k in range(2):
                    act.wait_ge(v_ready, tb * 2 + k + 1)
                    for n in range(2):
                        src = v_bank[k][:, n * E:(n + 1) * E].rearrange("p (h d) -> p h d", h=H)
                        nc.scalar.activation(v_all[:, tb * TPB + 2 * k + n, :, 0:D], src,
                                             ACT.Copy).then_inc(v_copied, 1)

            def cut(tb):
                for n, src, made in ((0, rot, rot_done), (1, rest, rest_done)):
                    act.wait_ge(piece_sent[n], tb * 64)
                    if n:
                        act.wait_ge(piece_done[2], tb * 4)
                    for u in range(4):
                        act.wait_ge(made, tb * 4 + u + 1)
                        nc.scalar.activation(piece[n][:, u, :], src[:, u, :], ACT.Copy).then_inc(piece_done[n], 1)

            act.wait_ge(const_ready, 3)
            project_copies(0)
            with act.Fori(0, NB - 1) as tb:
                project_copies(tb + 1)
                cut(tb)
            cut(NB - 1)

        @block.tensor
        def _(pe):
            pe.wait_ge(ident_ready, 2)
            pe.wait_ge(w_loaded, 64)
            with pe.Fori(0, NB) as tb:
                pe.wait_ge(xn_ready, tb * TPB + TPB)
                pe.wait_ge(xt_copied, tb * EC)
                for c in range(EC):
                    for k in range(TPB):
                        last = nc.tensor.transpose(x_bank[c][:, k * P:(k + 1) * P], xn[:, k, c * P:(c + 1) * P],
                                                   ident[:, :])
                    last.then_inc(xt_ready, 1)
                pe.wait_ge(xt_copied, tb * EC + EC)
                pe.wait_ge(v_copied, tb * TPB)
                for c in range(EC):
                    last = nc.tensor.matmul(lat_bank, w_lat[:, c, :], xn_t[:, c, :], start=c == 0, stop=c == EC - 1)
                last.then_inc(lat_ready, 1)
                pe.wait_ge(lat_copied, tb + 1)
                for k in range(TPB):
                    last = nc.tensor.matmul(v_bank[k // 2][:, (k % 2) * E:(k % 2 + 1) * E],
                                            lat_t[:, k * P:(k + 1) * P], w_v[:, :], start=True, stop=True)
                    if k % 2:
                        last.then_inc(v_ready, 1)
                pe.wait_ge(prod_done, tb * 8)
                for n in range(2):
                    for c in range(EC):
                        last = nc.tensor.matmul(qk_bank[0][n], w_q[:, c, n::2], xn_t[:, c, :],
                                                start=c == 0, stop=c == EC - 1)
                last.then_inc(qk_ready, 1)
                for n in range(2):
                    last = nc.tensor.matmul(qk_bank[1][n], w_k[:, n::2], lat_t[:, :], start=True, stop=True)
                last.then_inc(qk_ready, 1)

def max_units(b):
    units = [[(h, r, c, BLK, 0)] for c in range(b) for r in range(TPB) for h in range(G)]
    for r in range(TPB):
        keys = P * (r + 1)
        per = BLK // keys
        per = per if G % per == 0 else 1
        units += [[(h + n, r, b, keys, n * keys) for n in range(per)] for h in range(0, G, per)]
    return units

def attend(nc, ctx, io, keep, psum):
    def sb(name, shape, dt=F32):
        return ctx.enter_context(nc.sbuf_tensor(name, shape, dt))

    def sem(name):
        return ctx.enter_context(nc.semaphore(name))

    ident, v_all, attn = keep["ident"], keep["v_all"], keep["attn"]
    mask_row, ones = keep["mask_row"], keep["ones"]
    q_stack = sb("q_stack", [P, NB, H, BLK], BF16)
    k_stack = sb("k_stack", [P, NB, H, BLK], BF16)
    v_group = sb("v_group", [P, TILES, G, VW])
    probs = sb("probs", [P, 2, G, BLK])
    zeros = sb("zeros", [P, PAGE])
    out_t = sb("out_t", [P, NG, BLK])
    part_max = sb("part_max", [P, G, TPB, NB])
    neg_max = sb("neg_max", [P, G * TPB])
    shift = sb("shift", [G * TPB, SHIFT_ROWS, P], BF16)
    rsum = sb("rsum", [P, NG, TPB, G])

    s_bank = [banks(psum, h) for h in range(G)]
    m_bank = [banks(psum, 4), banks(psum, 5)]
    o_bank = banks(psum, 6)
    t_bank = [banks(psum, n) for n in (7, 4, 5, 6)]

    stack_loaded = [sem(f"stack_loaded{b}") for b in range(NB)]
    one_rows_set = sem("one_rows_set")
    zeros_set = sem("zeros_set")
    o_cleared = sem("o_cleared")
    m_ready = sem("m_ready")
    m_read = sem("m_read")
    neg_max_done = sem("neg_max_done")
    shift_done = sem("shift_done")
    shift_sent = sem("shift_sent")
    s_ready = sem("s_ready")
    exp_done = sem("exp_done")
    hidden = sem("hidden")
    v_staged = sem("v_staged")
    pv_done = sem("pv_done")
    o_copied = sem("o_copied")
    t_ready = sem("t_ready")
    rsum_done = sem("rsum_done")
    attn_done = sem("attn_done")

    units = [max_units(b) for b in range(NB)]
    steps = [TPB * (b + 1) for b in range(NB)]
    per_m = [len(u) + 1 for u in units]

    def m_base(b, g):
        return g * per_m[b] + NG * sum(per_m[:b])

    def s_base(b, g):
        return g * steps[b] + NG * sum(steps[:b])

    def index(b, g):
        return g + NG * b

    def first_col(b, s):
        return max(0, s - TPB * b) * P

    def m_slots(b, nxt):
        slots = max(steps[b] - TPB, 2)
        n = len(units[nxt])
        cuts = [n * (s + 1) // slots for s in range(slots)]
        return [cuts[0]] + [cuts[s] - cuts[s - 1] for s in range(1, slots)]

    with nc.Block() as block:

        @block.sync
        def _(sp):
            def load(b):
                d = [io["pieces"][s, b] for s in range(2)]
                row = H * BLK
                for n, rows in ((0, 3), (1, 2), (2, 1)):
                    at = sum(D * Q_PIECES.count(m) for m in range(n))
                    src = bass.AP(d[0].tensor, d[0].offset + n * D * row, [[0, rows], [row, D], [1, row]])
                    dst = q_stack[at:at + D * rows, b, :, :].rearrange("p h t -> p (h t)")
                    sp.dma_start(dst, src).then_inc(stack_loaded[b], 16)
                for at, rows in ((0, 3), (3, 2), (5, 1)):
                    src = bass.AP(d[1].tensor, d[1].offset, [[row, D * rows], [1, row]])
                    dst = k_stack[D * at:D * (at + rows), b, :, :].rearrange("p h t -> p (h t)")
                    sp.dma_start(dst, src).then_inc(stack_loaded[b], 16)

            def send_shift(b, g):
                sp.wait_ge(shift_done, index(b, g) * 2 + 2)
                for n in range(SHIFT_ROWS):
                    dst = q_stack[TERM_ROWS + n:TERM_ROWS + n + 1, b, bass.ds(g * G, G), :]
                    sp.dma_start(dst, shift[:, n, :]).then_inc(shift_sent, 16)

            load(0)
            send_shift(0, 0)
            for b in range(NB):
                if b + 1 < NB:
                    load(b + 1)
                with sp.Fori(0, NG - 1) as g:
                    send_shift(b, g + 1)
                if b + 1 < NB:
                    send_shift(b + 1, 0)
            sp.wait_ge(shift_sent, 16 * SHIFT_ROWS * NG * NB)

        @block.gpsimd
        def _(pool):
            one_bits = 0x3F803F80

            def set_ones(b):
                rows = k_stack[TERM_ROWS:STACK, b, :, :].rearrange("p h t -> p (h t)").bitcast(U32)
                nc.gpsimd.memset(rows, one_bits).then_inc(one_rows_set, 1)

            def group(b, g):
                pool.wait_ge(one_rows_set, min(b + 2, NB))
                pool.wait_ge(pv_done, s_base(b, g))
                nc.gpsimd.tensor_copy(v_group[:, 0:steps[b], :, :],
                                      v_all[:, 0:steps[b], bass.ds(g * G, G), :]).then_inc(v_staged, 1)
                for s in range(TPB * b, steps[b]):
                    pool.wait_ge(v_staged, index(b, g) + 1)
                    pool.wait_ge(exp_done, (s_base(b, g) + s + 1) * G)
                    col = first_col(b, s)
                    zero = zeros[PAGE:P, :].unsqueeze(1).to_broadcast([P - PAGE, G, PAGE])
                    nc.gpsimd.tensor_tensor(probs[PAGE:P, s % 2, :, col:col + PAGE], zero, zero,
                                            ALU.mult).then_inc(hidden, 1)

            nc.gpsimd.memset(zeros[:, :], 0.0).then_inc(zeros_set, 1)
            pool.wait_ge(zeros_set, 1)
            set_ones(0)
            for b in range(NB):
                if b + 1 < NB:
                    pool.wait_ge(hidden, NG * TPB * b)
                    set_ones(b + 1)
                with pool.Fori(0, NG) as g:
                    group(b, g)

        @block.vector
        def _(dve):
            nc.vector.memset(o_bank, 0.0).then_inc(o_cleared, 1)

            def read_max(b, g, n):
                dve.wait_ge(m_ready, m_base(b, g) + n + 1)
                unit = units[b][n]
                h, r, c, keys, _ = unit[0]
                m = len(unit)
                src = m_bank[n % 2][:, 0:m * keys].rearrange("p (m k) -> p m k", m=m)
                nc.vector.tensor_reduce(part_max[:, h:h + m, r, c:c + 1], src, axis=AX_X,
                                        op=ALU.max).then_inc(m_read, 1)

            def finish_max(b, g):
                n = len(units[b])
                dve.wait_ge(m_read, m_base(b, g) + n)
                nc.vector.tensor_reduce(neg_max[:, :], part_max[:, :, :, 0:b + 1], axis=AX_X, op=ALU.max,
                                        negate=True).then_inc(neg_max_done, 1)
                dve.wait_ge(m_ready, m_base(b, g) + n + 1)
                dve.wait_ge(shift_sent, index(b, g) * 16 * SHIFT_ROWS)
                rows = m_bank[n % 2][0:G * TPB, 0:P]
                nc.vector.tensor_copy(shift[:, 0, :], rows).then_inc(shift_done, 1)
                dve.wait_ge(shift_done, index(b, g) * 2 + 1)
                nc.vector.tensor_tensor(shift[:, 1, :], rows, shift[:, 0, :], ALU.subtract).then_inc(shift_done, 1)
                dve.wait_ge(shift_done, index(b, g) * 2 + 2)
                dve.sem_inc(m_read, 1)

            def maxima(b, g):
                dve.wait_ge(neg_max_done, index(b, g))
                for n in range(len(units[b])):
                    read_max(b, g, n)
                finish_max(b, g)

            maxima(0, 0)
            for b in range(NB):
                with dve.Fori(0, NG - 1) as g:
                    maxima(b, g + 1)
                if b + 1 < NB:
                    maxima(b + 1, 0)
                for g in range(NG):
                    dve.wait_ge(t_ready, index(b, g) + 1)
                    view = t_bank[g].rearrange("p (r h w) -> p r h w", r=TPB, h=G)
                    if b:
                        dve.wait_ge(attn_done, NG * b)
                    nc.vector.reciprocal(rsum[:, g, :, :], view[:, :, :, D]).then_inc(rsum_done, 1)
                for g in range(NG):
                    dve.wait_ge(rsum_done, index(b, g) + 1)
                    view = t_bank[g].rearrange("p (r h w) -> p r h w", r=TPB, h=G)
                    dst = attn[:, TPB * b:TPB * (b + 1), g * G * D:(g + 1) * G * D]
                    nc.vector.tensor_tensor(dst.rearrange("p r (h d) -> p r h d", h=G), view[:, :, :, 0:D],
                                            rsum[:, g, :, :].unsqueeze(3).to_broadcast([P, TPB, G, D]),
                                            ALU.mult).then_inc(attn_done, 1)

        @block.scalar
        def _(act):
            def group(b, g):
                for s in range(steps[b]):
                    n = s_base(b, g) + s
                    col = first_col(b, s)
                    if s >= 2:
                        act.wait_ge(pv_done, n - 1)
                    for h in range(G):
                        act.wait_ge(s_ready, n * G + h + 1)
                        nc.scalar.activation(probs[:, s % 2, h, col:BLK], s_bank[h][:, col:BLK], ACT.Exp,
                                             scale=ATTN_SCALE).then_inc(exp_done, 1)
                act.wait_ge(pv_done, s_base(b, g) + steps[b])
                act.wait_ge(t_ready, NG * b)
                nc.scalar.activation(out_t[:, g, :], o_bank, ACT.Copy).then_inc(o_copied, 1)

            for b in range(NB):
                with act.Fori(0, NG) as g:
                    group(b, g)

        @block.tensor
        def _(pe):
            def max_scores(b, g, n):
                if not (isinstance(g, int) and g == 0 and b == 0 and n < 2):
                    pe.wait_ge(m_read, m_base(b, g) + n - 1)
                bank = m_bank[n % 2]
                for h, r, c, keys, col in units[b][n]:
                    out = bank[:, col:col + keys]
                    diagonal = c == b
                    last = nc.tensor.matmul(out, q_stack[0:TERM_ROWS, b, g * G + h, r * P:(r + 1) * P],
                                            k_stack[0:TERM_ROWS, c, g * G + h, 0:keys],
                                            start=True, stop=not diagonal)
                    if diagonal:
                        last = nc.tensor.matmul(out[:, keys - PAGE:keys], mask_row[0:TERM_ROWS, :],
                                                ones[0:TERM_ROWS, :], start=False, stop=True)
                last.then_inc(m_ready, 1)

            def turn_max(b, g):
                n = len(units[b])
                pe.wait_ge(neg_max_done, index(b, g) + 1)
                pe.wait_ge(m_read, m_base(b, g) + n - 1)
                nc.tensor.transpose(m_bank[n % 2][0:G * TPB, 0:P], neg_max[:, :], ident[:, :]).then_inc(m_ready, 1)

            def scores(b, g, s):
                col = first_col(b, s)
                for h in range(G):
                    if s:
                        pe.wait_ge(exp_done, (s_base(b, g) + s - 1) * G + h + 1)
                    nc.tensor.matmul(s_bank[h][:, col:BLK],
                                     k_stack[0:STACK, s // TPB, g * G + h, (s % TPB) * P:(s % TPB + 1) * P],
                                     q_stack[0:STACK, b, g * G + h, col:BLK], start=True, stop=True)\
                        .then_inc(s_ready, 1)

            def weigh(b, g, s):
                n = s_base(b, g) + s
                col = first_col(b, s)
                pe.wait_ge(exp_done, n * G + G)
                if s >= TPB * b:
                    pe.wait_ge(hidden, index(b, g) * TPB + s - TPB * b + 1)
                if s == 0:
                    pe.wait_ge(v_staged, index(b, g) + 1)
                    pe.wait_ge(o_copied, index(b, g))
                    pe.wait_ge(attn_done, NG * b)
                for h in range(G):
                    last = nc.tensor.matmul(o_bank[32 * h:32 * h + VW, col:BLK], v_group[:, s, h, :],
                                            probs[:, s % 2, h, col:BLK], start=s == 0, stop=s == steps[b] - 1)
                last.then_inc(pv_done, 1)

            def group(b, g, nxt):
                slots = m_slots(b, nxt[0]) if nxt else []
                n = 0
                pe.wait_ge(shift_sent, (index(b, g) + 1) * 16 * SHIFT_ROWS)
                for s in range(steps[b]):
                    scores(b, g, s)
                    if s < len(slots):
                        if s == 0:
                            pe.wait_ge(attn_done, NG * b)
                        for _ in range(slots[s]):
                            max_scores(*nxt, n)
                            n += 1
                    if s:
                        weigh(b, g, s - 1)
                    if slots and s == len(slots) - 1:
                        turn_max(*nxt)
                weigh(b, g, steps[b] - 1)

            pe.wait_ge(o_cleared, 1)
            pe.wait_ge(stack_loaded[0], 96)
            for n in range(len(units[0])):
                max_scores(0, 0, n)
            turn_max(0, 0)
            for b in range(NB):
                pe.wait_ge(one_rows_set, b + 1)
                with pe.Fori(0, NG - 1) as g:
                    group(b, g, (b, g + 1))
                if b + 1 < NB:
                    pe.wait_ge(stack_loaded[b + 1], 96)
                group(b, NG - 1, (b + 1, 0) if b + 1 < NB else None)
                for g in range(NG):
                    pe.wait_ge(o_copied, index(b, g) + 1)
                    if g:
                        pe.wait_ge(m_read, m_base(b + 1, 0) + per_m[b + 1] if b + 1 < NB else m_base(b, NG))
                    for r in range(TPB):
                        last = nc.tensor.transpose(t_bank[g][:, r * P:(r + 1) * P], out_t[:, g, r * P:(r + 1) * P],
                                                   ident[:, :])
                    last.then_inc(t_ready, 1)

def fold(nc, ctx, io, keep, psum):
    def sb(name, shape, dt=F32):
        return ctx.enter_context(nc.sbuf_tensor(name, shape, dt))

    def sem(name):
        return ctx.enter_context(nc.semaphore(name))

    x, attn, ident = keep["x"], keep["attn"], keep["ident"]
    ctx_t, w_qk, bias_c, v_out = keep["ctx_t"], keep["w_qk"], keep["bias_c"], keep["v_out"]
    x2_t, row_fill, w_tern = keep["x2_t"], keep["row_fill"], keep["w_tern"]
    wo = sb("wo", [P, EC, E])
    cw_q = sb("cw_q", [P, HC, E + 1])
    cw_k = sb("cw_k", [P, HC, E])
    cw_v = sb("cw_v", [P, HC, E])
    cw_o = sb("cw_o", [P, HC, E])
    b_k = sb("b_k", [P, HC])
    b_v = sb("b_v", [P, HC])
    b_o = sb("b_o", [P, E])
    w_vo = sb("w_vo", [P, EC, E])
    row_w = sb("row_w", [P, E + 1])
    row_b = sb("row_b", [P, E])
    ffn_w = sb("ffn_w", [P, EC, E])
    abs_sum = sb("abs_sum", [P, 1])
    abs_all = sb("abs_all", [P, 1])
    limit = sb("limit", [P, 2])
    above = sb("above", [P, EC, E])
    attn_s = sb("attn_s", [P, TPB, E])
    attn_t = sb("attn_t", [P, EC, BLK])
    stats = sb("stats2", [P, TPB, 6])
    mv = sb("mv2", [P, TPB, 2])
    var = sb("var2", [P, TPB])
    rstd = sb("rstd2", [P, TPB])
    eps = sb("eps2", [P, TPB])
    minus_half = sb("minus_half2", [P, TPB])
    xn = sb("xn2", [P, TPB, E])
    dump = sb("dump", [P, E])
    dots = sb("dots", [P, TPB])

    a_bank = [banks(psum, 0), banks(psum, 1)]
    y_bank = [banks(psum, 2), banks(psum, 3)]
    n_bank = [banks(psum, 4), banks(psum, 5)]
    w_bank = [banks(psum, 6), banks(psum, 7)]

    att_w_loaded = sem("att_w_loaded")
    cross_w_loaded = sem("cross_w_loaded")
    ctx_loaded = sem("ctx_loaded")
    ffn_w_loaded = sem("ffn_w_loaded")
    set_done = sem("set_done")
    staged = sem("staged")
    a_ready = sem("a_ready")
    a_copied = sem("a_copied")
    y_ready = sem("y_ready")
    x_added = sem("x_added")
    stats_done = sem("stats_done2")
    waits_met = sem("waits_met2")
    mv_done = sem("mv_done2")
    var_done = sem("var_done2")
    rstd_done = sem("rstd_done2")
    xn_ready = sem("xn_ready2")
    dot_done = sem("dot_done")
    fill_done = sem("fill_done")
    bias_added = sem("bias_added")
    n_ready = sem("n_ready")
    n_copied = sem("n_copied")
    w_ready = sem("w_ready")
    w_copied = sem("w_copied")
    row_done = sem("row_done")
    tern_step = sem("tern_step")
    abs_ready = sem("abs_ready")
    abs_everywhere = sem("abs_everywhere")
    limit_done = sem("limit_done")

    V_FIRST = 7
    V_PAIRS = -(-S2_TILES // 2)
    N_W = V_FIRST + V_PAIRS

    with nc.Block() as block:

        @block.sync
        def _(sp):
            sp.dma_start(wo[:, :, :], io["wo"].rearrange("(c p) e -> p c e", p=P)).then_inc(att_w_loaded, 16)
            sp.dma_start(cw_q[:, :, 0:E], io["Wq"].rearrange("(c p) e -> p c e", p=P)).then_inc(cross_w_loaded, 16)
            sp.dma_start(cw_k[:, :, :], io["Wk"].rearrange("(c p) e -> p c e", p=P)).then_inc(cross_w_loaded, 16)
            sp.dma_start(cw_v[:, :, :], io["Wv"].rearrange("(c p) e -> p c e", p=P)).then_inc(cross_w_loaded, 16)
            sp.dma_start(cw_o[:, :, :], io["WoT"].rearrange("(c p) e -> p c e", p=P)).then_inc(cross_w_loaded, 16)
            with nc.allow_non_contiguous_dma(reason="bias vectors by partition"):
                sp.dma_start(cw_q[:, :, E:E + 1], io["bq"].rearrange("(c p o) -> p c o", p=P, o=1)).then_inc(cross_w_loaded, 16)
                sp.dma_start(b_k[:, :], io["bk"].rearrange("(c p) -> p c", p=P)).then_inc(cross_w_loaded, 16)
                sp.dma_start(b_v[:, :], io["bv"].rearrange("(c p) -> p c", p=P)).then_inc(cross_w_loaded, 16)
            sp.dma_start(b_o[:, :], bass.AP(io["bo"].tensor, 0, [[0, P], [1, E]])).then_inc(cross_w_loaded, 16)
            sp.dma_start(ctx_t[:, :, :], io["ctxT"].rearrange("(c p) s -> p c s", p=P)).then_inc(ctx_loaded, 16)
            sp.dma_start(ffn_w[:, :, :], io["ffn_w"].rearrange("(c p) e -> p c e", p=P)).then_inc(ffn_w_loaded, 16)

        @block.gpsimd
        def _(pool):
            nc.gpsimd.memset(eps[:, :], LN_EPS).then_inc(set_done, 1)
            nc.gpsimd.memset(minus_half[:, :], -0.5).then_inc(set_done, 1)
            pool.wait_ge(set_done, 2)

            def stage(tb):
                pool.wait_ge(a_ready, tb * EC)
                nc.gpsimd.tensor_copy(attn_s[:, :, :], attn[:, bass.ds(tb * TPB, TPB), :]).then_inc(staged, 1)

            def norm(tb):
                pool.wait_ge(mv_done, tb * TPB + TPB)
                nc.gpsimd.tensor_tensor(var[:, :], mv[:, :, 1], eps[:, :], ALU.add).then_inc(var_done, 1)
                pool.wait_ge(var_done, tb + 1)
                nc.gpsimd.tensor_tensor(rstd[:, :], var[:, :], minus_half[:, :], ALU.pow).then_inc(rstd_done, 1)
                pool.wait_ge(row_done, 2)
                pool.wait_ge(xn_ready, tb * TPB + TPB)
                tiles = x[:, bass.ds(tb * TPB, TPB), :]
                bias = row_b[:, :].unsqueeze(1).to_broadcast([P, TPB, E])
                nc.gpsimd.tensor_tensor(tiles, tiles, bias, ALU.add).then_inc(bias_added, 1)

            stage(0)
            with pool.Fori(0, NB - 1) as tb:
                stage(tb + 1)
                norm(tb)
            norm(NB - 1)
            pool.wait_ge(abs_ready, 1)
            nc.gpsimd.partition_all_reduce(abs_all[:, :], abs_sum[:, :], P, ReduceOp.add).then_inc(abs_everywhere, 1)

        @block.vector
        def _(dve):
            def rows():
                dve.wait_ge(w_ready, 5)
                nc.vector.tensor_copy(row_w[:, :], w_bank[0][:, 0:E + 1]).then_inc(row_done, 1)
                dve.wait_ge(w_ready, 6)
                dve.wait_ge(cross_w_loaded, 16 * 8)
                nc.vector.tensor_tensor(row_b[:, :], w_bank[1][:, 0:E], b_o[:, :], ALU.add).then_inc(row_done, 1)

            def block_of_tiles(tb):
                for k in range(2):
                    dve.wait_ge(y_ready, tb * 2 + k + 1)
                    tiles = x[:, bass.ds(tb * TPB + 2 * k, 2), :]
                    nc.vector.tensor_tensor(tiles, y_bank[k].rearrange("p (t e) -> p t e", t=2), tiles,
                                            ALU.add).then_inc(x_added, 1)
                dve.wait_ge(x_added, tb * 2 + 2)
                dve.sem_inc(waits_met, 1)
                for k in range(TPB):
                    nc.vector.bn_stats(out=stats[:, k, :], in_=x[:, tb * TPB + k, :]).then_inc(stats_done, 1)
                dve.wait_ge(stats_done, tb * TPB + TPB)
                dve.wait_ge(var_done, tb)
                dve.sem_inc(waits_met, 1)
                for k in range(TPB):
                    nc.vector.bn_aggr(out=mv[:, k, :], in_=stats[:, k, :]).then_inc(mv_done, 1)
                dve.wait_ge(rstd_done, tb + 1)
                dve.wait_ge(n_ready, tb * EC)
                for k in range(TPB):
                    nc.vector.tensor_scalar(xn[:, k, :], x[:, tb * TPB + k, :], mv[:, k, 0:1], rstd[:, k:k + 1],
                                            ALU.subtract, ALU.mult).then_inc(xn_ready, 1)
                for k in range(TPB):
                    dve.wait_ge(xn_ready, tb * TPB + k + 1)
                    dve.wait_ge(dot_done, tb * TPB + k)
                    nc.vector.tensor_tensor_reduce(out=dump[:, :], in0=xn[:, k, :], in1=row_w[:, 0:E], scale=1.0,
                                                   scalar=row_w[:, E:E + 1], op0=ALU.mult, op1=ALU.add,
                                                   accum_out=dots[:, k:k + 1]).then_inc(dot_done, 1)
                dve.wait_ge(dot_done, tb * TPB + TPB)
                nc.vector.tensor_scalar(row_fill[:, bass.ds(tb * TPB, TPB)], dots[:, :], -1.0, X_FILL,
                                        ALU.mult, ALU.add).then_inc(fill_done, 1)

            rows()
            dve.wait_ge(row_done, 2)
            with dve.Fori(0, NB) as tb:
                block_of_tiles(tb)
            dve.wait_ge(ffn_w_loaded, 16)
            nc.vector.tensor_reduce(abs_sum[:, :], ffn_w[:, :, :], axis=mybir.AxisListType.XY, op=ALU.add,
                                    apply_absolute_value=True).then_inc(abs_ready, 1)
            dve.wait_ge(abs_everywhere, 1)
            nc.vector.tensor_scalar(keep["beta"][:, :], abs_all[:, :], 1.0 / (E * E), None, ALU.mult).then_inc(limit_done, 1)
            dve.wait_ge(limit_done, 1)
            nc.vector.tensor_scalar(limit[:, 0:1], keep["beta"][:, :], FFN_EPS, 0.5, ALU.add, ALU.mult).then_inc(limit_done, 1)
            nc.vector.tensor_scalar(limit[:, 1:2], keep["beta"][:, :], FFN_EPS, -0.5, ALU.add, ALU.mult).then_inc(limit_done, 1)
            dve.wait_ge(limit_done, 3)
            nc.vector.tensor_scalar(above[:, :, :], ffn_w[:, :, :], limit[:, 0:1], None, ALU.is_gt).then_inc(tern_step, 1)
            nc.vector.tensor_scalar(ffn_w[:, :, :], ffn_w[:, :, :], limit[:, 1:2], None, ALU.is_lt).then_inc(tern_step, 1)
            dve.wait_ge(tern_step, 2)
            nc.vector.tensor_tensor(w_tern[:, :, :], above[:, :, :], ffn_w[:, :, :], ALU.subtract).then_inc(tern_step, 1)

        @block.scalar
        def _(act):
            def out(n, dst, src):
                act.wait_ge(w_ready, n + 1)
                nc.scalar.activation(dst, src, ACT.Copy).then_inc(w_copied, 1)

            for c in range(EC):
                out(c, w_qk[:, c, :], w_bank[c % 2][:, 0:E])
            for c in range(EC):
                out(2 + c, w_vo[:, c, :], w_bank[c % 2][:, 0:E])
            act.wait_ge(row_done, 2)
            out(6, bias_c[:, :], w_bank[0][:, 0:EC])
            for n in range(V_PAIRS):
                src = w_bank[(V_FIRST + n) % 2]
                for m in range(2):
                    j = 2 * n + m
                    if j < S2_TILES:
                        rows = P if j < S2_TILES - 1 else S2_TAIL
                        act.wait_ge(w_ready, V_FIRST + n + 1)
                        done = nc.scalar.activation(v_out[0:rows, j, :], src[0:rows, m * E:(m + 1) * E], ACT.Copy)
                done.then_inc(w_copied, 1)

            def turn_attn(tb):
                act.wait_ge(y_ready, tb * 2)
                for c in range(EC):
                    act.wait_ge(a_ready, tb * EC + c + 1)
                    nc.scalar.activation(attn_t[:, c, :], a_bank[c], ACT.Copy).then_inc(a_copied, 1)

            def turn_norm(tb):
                for c in range(EC):
                    act.wait_ge(n_ready, tb * EC + c + 1)
                    nc.scalar.activation(x2_t[:, c, tb, :], n_bank[c], ACT.Copy).then_inc(n_copied, 1)

            turn_attn(0)
            with act.Fori(0, NB - 1) as tb:
                turn_attn(tb + 1)
                turn_norm(tb)
            turn_norm(NB - 1)

        @block.tensor
        def _(pe):
            pe.wait_ge(cross_w_loaded, 16 * 8)
            for c in range(EC):
                for e in range(HC):
                    last = nc.tensor.matmul(w_bank[c][:, 0:E], cw_q[:, e, c * P:(c + 1) * P], cw_k[:, e, :],
                                            start=e == 0, stop=e == HC - 1)
                last.then_inc(w_ready, 1)
            for c in range(EC):
                pe.wait_ge(w_copied, c + 1)
                for e in range(HC):
                    last = nc.tensor.matmul(w_bank[c][:, 0:E], cw_v[:, e, c * P:(c + 1) * P], cw_o[:, e, :],
                                            start=e == 0, stop=e == HC - 1)
                last.then_inc(w_ready, 1)
            pe.wait_ge(w_copied, 3)
            for e in range(HC):
                last = nc.tensor.matmul(w_bank[0][:, 0:E + 1], b_k[:, e:e + 1].to_broadcast([P, P]), cw_q[:, e, :],
                                        start=e == 0, stop=e == HC - 1)
            last.then_inc(w_ready, 1)
            pe.wait_ge(w_copied, 4)
            for e in range(HC):
                last = nc.tensor.matmul(w_bank[1][:, 0:E], b_v[:, e:e + 1].to_broadcast([P, P]), cw_o[:, e, :],
                                        start=e == 0, stop=e == HC - 1)
            last.then_inc(w_ready, 1)
            pe.wait_ge(row_done, 1)
            for c in range(EC):
                for e in range(HC):
                    last = nc.tensor.matmul(w_bank[0][:, c:c + 1], cw_k[:, e, c * P:(c + 1) * P], cw_q[:, e, E:E + 1],
                                            start=e == 0, stop=e == HC - 1)
            last.then_inc(w_ready, 1)
            pe.wait_ge(ctx_loaded, 16)
            for n in range(V_PAIRS):
                pe.wait_ge(row_done, 2)
                if n >= 1:
                    pe.wait_ge(w_copied, n + 4)
                for j in range(2 * n, min(2 * n + 2, S2_TILES)):
                    keys = P if j < S2_TILES - 1 else S2_TAIL
                    dst = w_bank[(V_FIRST + n) % 2][0:keys, (j % 2) * E:(j % 2 + 1) * E]
                    for c in range(EC):
                        last = nc.tensor.matmul(dst, ctx_t[:, c, j * P:j * P + keys], w_vo[:, c, :],
                                                start=c == 0, stop=c == EC - 1)
                last.then_inc(w_ready, 1)
            pe.wait_ge(att_w_loaded, 16)

            def output(tb):
                pe.wait_ge(staged, tb + 1)
                pe.wait_ge(a_copied, tb * EC)
                for c in range(EC):
                    for k in range(TPB):
                        last = nc.tensor.transpose(a_bank[c][:, k * P:(k + 1) * P], attn_s[:, k, c * P:(c + 1) * P],
                                                   ident[:, :])
                    last.then_inc(a_ready, 1)
                pe.wait_ge(a_copied, tb * EC + EC)
                pe.wait_ge(x_added, tb * 2)
                for k in range(TPB):
                    for c in range(EC):
                        last = nc.tensor.matmul(y_bank[k // 2][:, (k % 2) * E:(k % 2 + 1) * E],
                                                attn_t[:, c, k * P:(k + 1) * P], wo[:, c, :],
                                                start=c == 0, stop=c == EC - 1)
                    if k % 2:
                        last.then_inc(y_ready, 1)

            def normed(tb):
                pe.wait_ge(xn_ready, tb * TPB + TPB)
                pe.wait_ge(n_copied, tb * EC)
                for c in range(EC):
                    for k in range(TPB):
                        last = nc.tensor.transpose(n_bank[c][:, k * P:(k + 1) * P], xn[:, k, c * P:(c + 1) * P],
                                                   ident[:, :])
                    last.then_inc(n_ready, 1)

            output(0)
            with pe.Fori(0, NB - 1) as tb:
                output(tb + 1)
                normed(tb)
            normed(NB - 1)

def cross(nc, ctx, io, keep, psum):
    def sb(name, shape, dt=F32):
        return ctx.enter_context(nc.sbuf_tensor(name, shape, dt))

    def sem(name):
        return ctx.enter_context(nc.semaphore(name))

    x, ident = keep["x"], keep["ident"]
    ctx_t, w_qk, bias_c, v_out = keep["ctx_t"], keep["w_qk"], keep["bias_c"], keep["v_out"]
    x2_t, row_fill, x3, abs_max = keep["x2_t"], keep["row_fill"], keep["x3"], keep["abs_max"]
    mask = sb("mask", [P, 2, S2], I32)
    zeros = sb("zeros_s2", [P, S2])
    qc_t = sb("qc_t", [P, 2, EC, P])
    e = sb("e", [P, 2, S2])
    neg = sb("neg", [P, 2])
    esum = sb("esum", [P, 2])
    rsum = sb("rsum_x", [P, 2])
    p_t = sb("p_t", [P, S2_TILES, P])
    gamma = sb("gamma", [P, E])
    beta = sb("beta_row", [P, E])
    stats = sb("stats3", [P, 6])
    mv = sb("mv3", [P, 2])
    va = sb("va", [P, 1])
    ra = sb("ra", [P, 1])
    rr = sb("rr", [P, 1])
    vb = sb("vb", [P, 1])
    vc = sb("vc", [P, 1])
    rb = sb("rb", [P, 1])
    scale = sb("scale3", [P, 1])
    consts = sb("consts3", [P, 3])
    z = sb("z", [P, E])
    zg = sb("zg", [P, E])

    CHUNKS = [(c * TPB, min(TPB, S2_TILES - c * TPB)) for c in range(-(-S2_TILES // TPB))]
    NCH = len(CHUNKS)
    e_bank = psum[:, 0:S2]
    t_bank = [banks(psum, 4), banks(psum, 5)]
    y_bank = banks(psum, 6)
    q_bank = banks(psum, 7)

    mask_loaded = [sem(f"mask_loaded{n}") for n in range(2)]
    rows_loaded = sem("rows_loaded")
    set_done = sem("set_done3")
    qc_ready = sem("qc_ready")
    qc_copied = sem("qc_copied")
    filled = sem("filled")
    e_ready = sem("e_ready")
    e_taken = sem("e_taken")
    max_done = sem("max_done")
    exp_done = sem("exp_done3")
    t_ready = sem("t_ready3")
    t_copied_a = sem("t_copied_a")
    t_copied_v = sem("t_copied_v")
    y_ready = sem("y_ready3")
    rsum_done = sem("rsum_done3")
    x_added = sem("x_added3")
    stats_done = sem("stats_done3")
    mv_done = sem("mv_done3")
    pool_step = sem("pool_step")
    z_done = sem("z_done")
    zg_done = sem("zg_done")
    xn3_done = sem("xn3_done")
    abs_done = sem("abs_done")
    waits_met = sem("waits_met3")
    POOL_STEPS = 7

    PAIRS = TILES // 2

    def pairs(engine, body, first=None):
        with engine.Fori(0, PAIRS - 1) as k:
            for h in range(2):
                body(2 * k + h, h, False)
        for h in range(2):
            body(2 * (PAIRS - 1) + h, h, h == 1)

    with nc.Block() as block:

        @block.sync
        def _(sp):
            sp.dma_start(gamma[:, :], bass.AP(io["gamma"].tensor, 0, [[0, P], [1, E]])).then_inc(rows_loaded, 16)
            sp.dma_start(beta[:, :], bass.AP(io["beta"].tensor, 0, [[0, P], [1, E]])).then_inc(rows_loaded, 16)
            masks = io["mask"].rearrange("(t p) s -> t p s", p=P)
            for h in range(2):
                sp.dma_start(mask[:, h, :], masks[h]).then_inc(mask_loaded[h], 16)
            with sp.Fori(0, PAIRS - 1) as k:
                for h in range(2):
                    sp.wait_ge(e_taken, 2 * k + h + 1)
                    sp.dma_start(mask[:, h, :], masks[2 * k + (h + 2)]).then_inc(mask_loaded[h], 16)

        @block.gpsimd
        def _(pool):
            nc.gpsimd.memset(zeros[:, :], 0.0).then_inc(set_done, 1)
            for n, value in enumerate((LN_EPS, FFN_LN_EPS, -0.5)):
                nc.gpsimd.memset(consts[:, n:n + 1], value).then_inc(set_done, 1)
            pool.wait_ge(set_done, 4)

            def body(i, h, last):
                if not last:
                    pool.wait_ge(t_ready, i * NCH)
                    nc.gpsimd.tensor_tensor(e[:, 1 - h, :], zeros[:, :],
                                            row_fill[:, bass.ds(i + 1, 1)].to_broadcast([P, S2]),
                                            ALU.add).then_inc(filled, 1)
                pool.wait_ge(mv_done, i + 1)
                n = i * POOL_STEPS
                nc.gpsimd.tensor_tensor(va[:, :], mv[:, 1:2], consts[:, 0:1], ALU.add).then_inc(pool_step, 1)
                pool.wait_ge(pool_step, n + 1)
                nc.gpsimd.tensor_tensor(ra[:, :], va[:, :], consts[:, 2:3], ALU.pow).then_inc(pool_step, 1)
                pool.wait_ge(pool_step, n + 2)
                nc.gpsimd.tensor_tensor(rr[:, :], ra[:, :], ra[:, :], ALU.mult).then_inc(pool_step, 1)
                pool.wait_ge(pool_step, n + 3)
                nc.gpsimd.tensor_tensor(vb[:, :], rr[:, :], mv[:, 1:2], ALU.mult).then_inc(pool_step, 1)
                pool.wait_ge(pool_step, n + 4)
                nc.gpsimd.tensor_tensor(vc[:, :], vb[:, :], consts[:, 1:2], ALU.add).then_inc(pool_step, 1)
                pool.wait_ge(pool_step, n + 5)
                nc.gpsimd.tensor_tensor(rb[:, :], vc[:, :], consts[:, 2:3], ALU.pow).then_inc(pool_step, 1)
                pool.wait_ge(pool_step, n + 6)
                nc.gpsimd.tensor_tensor(scale[:, :], ra[:, :], rb[:, :], ALU.mult).then_inc(pool_step, 1)
                pool.wait_ge(xn3_done, i)
                pool.wait_ge(z_done, i + 1)
                nc.gpsimd.tensor_tensor(zg[:, :], z[:, :], gamma[:, :], ALU.mult).then_inc(zg_done, 1)
                pool.wait_ge(zg_done, i + 1)
                nc.gpsimd.tensor_tensor(x3[:, bass.ds(i, 1), :].rearrange("p o e -> p (o e)"), zg[:, :], beta[:, :], ALU.add).then_inc(xn3_done, 1)

            pool.wait_ge(rows_loaded, 32)
            nc.gpsimd.tensor_tensor(e[:, 0, :], zeros[:, :], row_fill[:, 0:1].to_broadcast([P, S2]),
                                    ALU.add).then_inc(filled, 1)
            pool.wait_ge(filled, 1)
            pairs(pool, body)

        @block.vector
        def _(dve):
            def take(i, h):
                dve.wait_ge(mask_loaded[h], (i - h) * 8 + 16)
                dve.wait_ge(filled, i + 1)
                dve.wait_ge(e_ready, i + 1)
                dve.sem_inc(waits_met, 1)
                nc.vector.copy_predicated(e[:, h, :], mask[:, h, :], e_bank).then_inc(e_taken, 1)
                dve.wait_ge(e_taken, i + 1)
                nc.vector.tensor_reduce(neg[:, h:h + 1], e[:, h, :], axis=AX_X, op=ALU.max).then_inc(max_done, 1)
                dve.wait_ge(max_done, 2 * i + 1)
                nc.vector.tensor_scalar(neg[:, h:h + 1], neg[:, h:h + 1], -X_SCALE, None,
                                        ALU.mult).then_inc(max_done, 1)

            def body(i, h, last):
                for n, (j, m) in enumerate(CHUNKS):
                    if n % 2:
                        rows = P if n < NCH - 1 else S2_TAIL
                        dve.wait_ge(y_ready, i)
                        dve.wait_ge(t_ready, i * NCH + n + 1)
                        nc.vector.tensor_copy(p_t[0:rows, j:j + m, :].rearrange("p j q -> p (j q)"),
                                              t_bank[1][0:rows, 0:m * P]).then_inc(t_copied_v, 1)
                if not last:
                    take(i + 1, 1 - h)
                dve.wait_ge(exp_done, i + 1)
                nc.vector.reciprocal(rsum[:, h:h + 1], esum[:, h:h + 1]).then_inc(rsum_done, 1)
                dve.wait_ge(rsum_done, i + 1)
                dve.wait_ge(y_ready, i + 1)
                nc.vector.scalar_tensor_tensor(out=x[:, i, :], in0=y_bank[:, 0:E], scalar=rsum[:, h:h + 1],
                                               in1=x[:, i, :], op0=ALU.mult, op1=ALU.add).then_inc(x_added, 1)
                dve.wait_ge(x_added, i + 1)
                dve.sem_inc(waits_met, 1)
                nc.vector.bn_stats(out=stats[:, :], in_=x[:, i, :]).then_inc(stats_done, 1)
                dve.wait_ge(stats_done, i + 1)
                dve.wait_ge(pool_step, i * POOL_STEPS)
                dve.sem_inc(waits_met, 1)
                nc.vector.bn_aggr(out=mv[:, :], in_=stats[:, :]).then_inc(mv_done, 1)
                dve.wait_ge(pool_step, i * POOL_STEPS + POOL_STEPS)
                dve.wait_ge(zg_done, i)
                nc.vector.tensor_scalar(z[:, :], x[:, i, :], mv[:, 0:1], scale[:, :],
                                        ALU.subtract, ALU.mult).then_inc(z_done, 1)
                dve.wait_ge(xn3_done, i + 1)
                nc.vector.tensor_reduce(abs_max[:, bass.ds(i, 1)], x3[:, i, :], axis=AX_X, op=ALU.max,
                                        apply_absolute_value=True).then_inc(abs_done, 1)

            take(0, 0)
            pairs(dve, body)

        @block.scalar
        def _(act):
            def prepare(i, h):
                act.wait_ge(qc_ready, i + 1)
                for c in range(EC):
                    nc.scalar.activation(qc_t[:, h, c, :], q_bank[:, c * P:(c + 1) * P], ACT.Identity,
                                         bias=bias_c[:, c:c + 1]).then_inc(qc_copied, 1)

            def exponential(i, h):
                act.wait_ge(max_done, 2 * i + 2)
                nc.scalar.activation(e[:, h, :], e[:, h, :], ACT.Exp, scale=X_SCALE, bias=neg[:, h:h + 1],
                                     accum_out=esum[:, h:h + 1]).then_inc(exp_done, 1)

            def body(i, h, last):
                if not last:
                    prepare(i + 1, 1 - h)
                for n, (j, m) in enumerate(CHUNKS):
                    if n % 2 == 0:
                        act.wait_ge(y_ready, i)
                        act.wait_ge(t_ready, i * NCH + n + 1)
                        nc.scalar.activation(p_t[:, j:j + m, :].rearrange("p j q -> p (j q)"),
                                             t_bank[0][:, 0:m * P], ACT.Copy).then_inc(t_copied_a, 1)
                if not last:
                    act.wait_ge(rsum_done, i)
                    exponential(i + 1, 1 - h)

            prepare(0, 0)
            exponential(0, 0)
            pairs(act, body)

        @block.tensor
        def _(pe):
            def score(i, h):
                pe.wait_ge(qc_copied, i * EC)
                for c in range(EC):
                    for k in range(EC):
                        last = nc.tensor.matmul(q_bank[:, c * P:(c + 1) * P], w_qk[:, k, c * P:(c + 1) * P],
                                                x2_t[:, k, :, :].rearrange("p b t -> p (b t)")[:, bass.ds(i * P, P)],
                                                start=k == 0, stop=k == EC - 1)
                last.then_inc(qc_ready, 1)
                pe.wait_ge(e_taken, i)
                pe.wait_ge(qc_copied, (i + 1) * EC)
                for c0 in range(0, S2, BLK):
                    c1 = min(c0 + BLK, S2)
                    for k in range(EC):
                        last = nc.tensor.matmul(e_bank[:, c0:c1], qc_t[:, h, k, :], ctx_t[:, k, c0:c1],
                                                start=k == 0, stop=k == EC - 1)
                last.then_inc(e_ready, 1)

            def body(i, h, last):
                if not last:
                    score(i + 1, 1 - h)
                pe.wait_ge(exp_done, i + 1)
                for n, (j0, m) in enumerate(CHUNKS):
                    if n >= 2:
                        if n % 2:
                            pe.wait_ge(t_copied_v, i * (NCH // 2) + n // 2)
                        else:
                            pe.wait_ge(t_copied_a, i * (NCH - NCH // 2) + n // 2)
                    for j in range(j0, j0 + m):
                        keys = P if j < S2_TILES - 1 else S2_TAIL
                        last_t = nc.tensor.transpose(t_bank[n % 2][0:keys, (j - j0) * P:(j - j0 + 1) * P],
                                                     e[:, h, j * P:j * P + keys], ident[:, :])
                    last_t.then_inc(t_ready, 1)
                pe.wait_ge(x_added, i)
                for n, (j0, m) in enumerate(CHUNKS):
                    if n % 2:
                        pe.wait_ge(t_copied_v, i * (NCH // 2) + n // 2 + 1)
                    else:
                        pe.wait_ge(t_copied_a, i * (NCH - NCH // 2) + n // 2 + 1)
                    for j in range(j0, j0 + m):
                        keys = P if j < S2_TILES - 1 else S2_TAIL
                        mm = nc.tensor.matmul(y_bank[:, 0:E], p_t[0:keys, j, :], v_out[0:keys, j, :],
                                              start=j == 0, stop=j == S2_TILES - 1)
                mm.then_inc(y_ready, 1)

            score(0, 0)
            pairs(pe, body)

def feed(nc, ctx, io, keep, psum):
    def sb(name, shape, dt=F32):
        return ctx.enter_context(nc.sbuf_tensor(name, shape, dt))

    def sem(name):
        return ctx.enter_context(nc.semaphore(name))

    x, x3, ident, w_tern = keep["x"], keep["x3"], keep["ident"], keep["w_tern"]
    top = sb("top", [P, 1])
    top_all = sb("top_all", [P, 1])
    to_q = sb("to_q", [P, 1])
    back_1 = sb("back_1", [P, 1])
    back = sb("back", [P, 1])
    scaled = sb("scaled", [P, TPB, E])
    xq = sb("xq", [P, TPB, E])
    xq_t = sb("xq_t", [P, EC, BLK])
    y = sb("y", [P, 2, TPB, E])

    x_bank = [banks(psum, 0), banks(psum, 1)]
    y_bank = [banks(psum, 2), banks(psum, 3)]

    top_done = sem("top_done")
    top_everywhere = sem("top_everywhere")
    factor_done = sem("factor_done")
    scaled_done = sem("scaled_done")
    xq_done = sem("xq_done")
    xt_ready = sem("xt_ready4")
    xt_copied = sem("xt_copied4")
    y_ready = sem("y_ready4")
    y_added = sem("y_added")
    y_sent = [sem(f"y_sent{n}") for n in range(2)]

    with nc.Block() as block:

        @block.sync
        def _(sp):
            out = io["out"].rearrange("(b t p) e -> b p t e", p=P, t=TPB)
            for tb in range(NB):
                sp.wait_ge(y_added, tb * TPB + TPB)
                sp.dma_start(out[tb], y[:, tb % 2, :, :]).then_inc(y_sent[tb % 2], 16)
            for n in range(2):
                sp.wait_ge(y_sent[n], 16 * NB // 2)

        @block.gpsimd
        def _(pool):
            pool.wait_ge(top_done, 1)
            nc.gpsimd.partition_all_reduce(top_all[:, :], top[:, :], P, ReduceOp.max).then_inc(top_everywhere, 1)

        @block.vector
        def _(dve):
            nc.vector.tensor_reduce(top[:, :], keep["abs_max"][:, :], axis=AX_X, op=ALU.max).then_inc(top_done, 1)
            dve.wait_ge(top_everywhere, 1)
            nc.vector.reciprocal(to_q[:, :], top_all[:, :]).then_inc(factor_done, 1)
            nc.vector.tensor_tensor(back_1[:, :], top_all[:, :], keep["beta"][:, :], ALU.mult).then_inc(factor_done, 1)
            dve.wait_ge(factor_done, 2)
            nc.vector.tensor_scalar(to_q[:, :], to_q[:, :], QB, None, ALU.mult).then_inc(factor_done, 1)
            nc.vector.tensor_scalar(back[:, :], back_1[:, :], 1.0 / QB, None, ALU.mult).then_inc(factor_done, 1)
            dve.wait_ge(factor_done, 4)

            def clip(tb):
                dve.wait_ge(xt_ready, tb * EC)
                dve.wait_ge(scaled_done, tb + 1)
                nc.vector.tensor_scalar(xq[:, :, :], scaled[:, :, :], QB - FFN_EPS, FFN_EPS - QB,
                                        ALU.min, ALU.max).then_inc(xq_done, 1)

            def add(tb):
                if tb >= 2:
                    dve.wait_ge(y_sent[tb % 2], tb // 2 * 16)
                for k in range(TPB):
                    dve.wait_ge(y_ready, tb * 2 + k // 2 + 1)
                    nc.vector.scalar_tensor_tensor(out=y[:, tb % 2, k, :], in0=y_bank[k // 2][:, (k % 2) * E:(k % 2 + 1) * E],
                                                   scalar=back[:, :], in1=x[:, tb * TPB + k, :],
                                                   op0=ALU.mult, op1=ALU.add).then_inc(y_added, 1)

            clip(0)
            for tb in range(NB):
                if tb + 1 < NB:
                    clip(tb + 1)
                add(tb)

        @block.scalar
        def _(act):
            act.wait_ge(factor_done, 4)
            for tb in range(NB):
                act.wait_ge(xq_done, tb)
                nc.scalar.activation(scaled[:, :, :], x3[:, tb * TPB:(tb + 1) * TPB, :], ACT.Copy,
                                     scale=to_q[:, :]).then_inc(scaled_done, 1)
                act.wait_ge(y_ready, tb * 2)
                for c in range(EC):
                    act.wait_ge(xt_ready, tb * EC + c + 1)
                    nc.scalar.activation(xq_t[:, c, :], x_bank[c], ACT.Copy).then_inc(xt_copied, 1)

        @block.tensor
        def _(pe):
            for tb in range(NB):
                pe.wait_ge(xq_done, tb + 1)
                pe.wait_ge(xt_copied, tb * EC)
                for c in range(EC):
                    for k in range(TPB):
                        last = nc.tensor.transpose(x_bank[c][:, k * P:(k + 1) * P], xq[:, k, c * P:(c + 1) * P],
                                                   ident[:, :])
                    last.then_inc(xt_ready, 1)
                pe.wait_ge(xt_copied, tb * EC + EC)
                pe.wait_ge(y_added, tb * TPB)
                for k in range(TPB):
                    for c in range(EC):
                        last = nc.tensor.matmul(y_bank[k // 2][:, (k % 2) * E:(k % 2 + 1) * E],
                                                xq_t[:, c, k * P:(k + 1) * P], w_tern[:, c, :],
                                                start=c == 0, stop=c == EC - 1)
                    if k % 2:
                        last.then_inc(y_ready, 1)

def build(nc, io):
    with ExitStack() as outer:
        def sb(name, shape, dt=F32):
            return outer.enter_context(nc.sbuf_tensor(name, shape, dt))

        psum = outer.enter_context(nc.psum_tensor("psum", [P, 8 * BLK], F32))
        keep = {"x": sb("x_sb", [P, TILES, E]), "ident": sb("ident", [P, P])}
        with ExitStack() as own:
            def sbo(name, shape, dt=F32):
                return own.enter_context(nc.sbuf_tensor(name, shape, dt))

            keep["attn"] = sbo("attn", [P, TILES, E])
            with ExitStack() as early:
                def sbe(name, shape, dt=F32):
                    return early.enter_context(nc.sbuf_tensor(name, shape, dt))

                keep["v_all"] = sbe("v_all", [P, TILES, H, VW])
                keep["mask_row"] = sbe("mask_row", [P, P], BF16)
                keep["ones"] = sbe("ones", [P, PAGE], BF16)
                with ExitStack() as ctx:
                    project(nc, ctx, io, keep, psum)
                with ExitStack() as ctx:
                    attend(nc, ctx, io, keep, psum)
            keep["x2_t"] = sbo("x2_t", [P, EC, NB, BLK])
            keep["row_fill"] = sbo("row_fill", [P, TILES])
            keep["ctx_t"] = sbo("ctx_t", [P, EC, S2])
            keep["w_qk"] = sbo("w_qk", [P, EC, E])
            keep["bias_c"] = sbo("bias_c", [P, EC])
            keep["v_out"] = sbo("v_out", [P, S2_TILES, E])
            keep["w_tern"] = sbo("w_tern", [P, EC, E])
            keep["beta"] = sbo("beta", [P, 1])
            keep["abs_max"] = sbo("abs_max", [P, TILES])
            with ExitStack() as ctx:
                fold(nc, ctx, io, keep, psum)
            keep["x3"] = keep["attn"]
            with ExitStack() as ctx:
                cross(nc, ctx, io, keep, psum)
            with ExitStack() as ctx:
                feed(nc, ctx, io, keep, psum)

def rope_tables():
    import numpy as np

    inv = 1.0 / 10000.0 ** (np.arange(0, D, 2, dtype=np.float32) / D)
    ang = np.outer(np.arange(T, dtype=np.float32), inv)
    return (np.ascontiguousarray(np.cos(ang).astype(np.float32).T),
            np.ascontiguousarray(np.sin(ang).astype(np.float32).T))

def kernel(x, ctx_1024, mask_BxSxS2_ik1, L0_attn_wq, L0_attn_w_down, L0_attn_wk_up, L0_attn_wv_up, L0_attn_wo,
           L0_xattn_Wq, L0_xattn_bq, L0_xattn_Wk, L0_xattn_bk, L0_xattn_Wv, L0_xattn_bv, L0_xattn_Wo, L0_xattn_bo,
           L0_ffn_weight, L0_ffn_ln_gamma, L0_ffn_ln_beta):
    import numpy as np
    import concourse.bacc as bacc
    from concourse.bass_utils import run_bass_kernel_spmd

    cos, sin = rope_tables()
    arrays = {
        "x": np.asarray(x)[0], "wq": L0_attn_wq, "w_down": L0_attn_w_down, "wk_up": L0_attn_wk_up,
        "wv_up": L0_attn_wv_up, "wo": L0_attn_wo, "cos": cos, "sin": sin,
        "ctxT": np.asarray(ctx_1024)[0].T, "mask": np.asarray(mask_BxSxS2_ik1)[0],
        "Wq": L0_xattn_Wq, "Wk": L0_xattn_Wk, "Wv": L0_xattn_Wv, "WoT": np.asarray(L0_xattn_Wo).T,
        "bq": L0_xattn_bq, "bk": L0_xattn_bk, "bv": L0_xattn_bv, "bo": L0_xattn_bo,
        "ffn_w": L0_ffn_weight, "gamma": L0_ffn_ln_gamma, "beta": L0_ffn_ln_beta,
    }
    arrays = {name: np.ascontiguousarray(a) for name, a in arrays.items()}
    nc = bacc.Bacc("TRN2", target_bir_lowering=False, num_devices=1)
    io = {name: nc.dram_tensor("in_" + name, a.shape, mybir.dt.from_np(a.dtype), kind="ExternalInput").ap()
          for name, a in arrays.items()}
    io["pieces"] = nc.dram_tensor("pieces", (2, NB, 3, 2, HALF, H, BLK), BF16, kind="Internal").ap()
    io["out"] = nc.dram_tensor("out", (T, E), F32, kind="ExternalOutput").ap()
    build(nc, io)
    got = run_bass_kernel_spmd(nc, [{"in_" + name: a for name, a in arrays.items()}], core_ids=[0])
    return got.results[0]["out"].reshape(1, T, E)
```

```python
from contextlib import ExitStack

import concourse.bass as bass
from concourse import mybir

F32 = mybir.dt.float32
BF16 = mybir.dt.bfloat16
I32 = mybir.dt.int32
U32 = mybir.dt.uint32
ALU = mybir.AluOpType
ACT = mybir.ActivationFunctionType
AX_X = mybir.AxisListType.X
ReduceOp = bass.bass_isa.ReduceOp

P = 128
T, E = 2048, 256
EC = E // P
H, D = 16, 16
HALF = D // 2
TILES = T // P
BLK = 512
NB = T // BLK
TPB = BLK // P
PAGE = 64
G = 4
NG = H // G
VW = D + 1
LN_EPS = 1e-5
ATTN_SCALE = float(D) ** -0.5
NEG_BIG = -1e30

Q_PIECES = [0, 0, 0, 1, 1, 2]
K_PIECES = [0, 1, 2, 0, 1, 0]
TERM_ROWS = D * len(Q_PIECES)
SHIFT_ROWS = 2
STACK = TERM_ROWS + SHIFT_ROWS

S2 = 1601
S2_TILES = -(-S2 // P)
S2_TAIL = S2 - (S2_TILES - 1) * P
DH = 1024
HC = DH // P
X_SCALE = float(DH) ** -0.5
X_FILL = -(2.0 ** 15) / X_SCALE

QB, FFN_EPS, FFN_LN_EPS = 128.0, 1e-5, 1e-3

def banks(psum, first, n=1):
    return psum[:, first * BLK:(first + n) * BLK]

def project(nc, ctx, io, keep, psum):
    def sb(name, shape, dt=F32):
        return ctx.enter_context(nc.sbuf_tensor(name, shape, dt))

    def sem(name):
        return ctx.enter_context(nc.semaphore(name))

    x, ident, v_all = keep["x"], keep["ident"], keep["v_all"]
    w_q = sb("w_q", [P, EC, E])
    w_lat = sb("w_lat", [P, EC, P])
    w_k = sb("w_k", [P, E])
    w_v = sb("w_v", [P, E])
    cos = sb("cos", [P, NB, BLK])
    sin = sb("sin", [P, NB, BLK])
    stats = sb("stats", [P, TPB, 6])
    mv = sb("mv", [P, TPB, 2])
    var = sb("var", [P, TPB])
    rstd = sb("rstd", [P, TPB])
    minus_half = sb("minus_half", [P, TPB])
    eps = sb("eps", [P, TPB])
    xn = sb("xn", [P, TPB, E])
    xn_t = sb("xn_t", [P, EC, BLK])
    lat_t = sb("lat_t", [P, BLK])
    prod_a = sb("prod_a", [P, 4, BLK])
    prod_b = sb("prod_b", [P, 4, BLK])
    rot = sb("rot", [P, 4, BLK])
    rest = sb("rest", [P, 4, BLK])
    piece = [sb(f"piece{n}", [P, 4, BLK], BF16) for n in range(3)]

    x_bank = [banks(psum, 0), banks(psum, 1)]
    lat_bank = banks(psum, 2)
    v_bank = [banks(psum, 2), banks(psum, 3)]
    qk_bank = [[banks(psum, 4), banks(psum, 5)], [banks(psum, 6), banks(psum, 7)]]

    x_loaded = sem("x_loaded")
    w_loaded = sem("w_loaded")
    rope_loaded = sem("rope_loaded")
    ident_ready = sem("ident_ready")
    const_ready = sem("const_ready")
    stats_done = sem("stats_done")
    waits_met = sem("waits_met")
    mv_done = sem("mv_done")
    var_done = sem("var_done")
    rstd_done = sem("rstd_done")
    xn_ready = sem("xn_ready")
    xt_ready = sem("xt_ready")
    xt_copied = sem("xt_copied")
    lat_ready = sem("lat_ready")
    lat_copied = sem("lat_copied")
    v_ready = sem("v_ready")
    v_copied = sem("v_copied")
    qk_ready = sem("qk_ready")
    prod_done = sem("prod_done")
    rot_done = sem("rot_done")
    rest_done = sem("rest_done")
    piece_done = [sem(f"piece_done{n}") for n in range(3)]
    piece_sent = [sem(f"piece_sent{n}") for n in range(3)]

    with nc.Block() as block:

        @block.sync
        def _(sp):
            sp.dma_start(x[:, :, :], io["x"].rearrange("(t p) e -> p t e", p=P)).then_inc(x_loaded, 16)
            sp.dma_start(w_q[:, :, :], io["wq"].rearrange("(c p) e -> p c e", p=P)).then_inc(w_loaded, 16)
            sp.dma_start(w_lat[:, :, :], io["w_down"].rearrange("(c p) e -> p c e", p=P)).then_inc(w_loaded, 16)
            sp.dma_start(w_k[:, :], io["wk_up"]).then_inc(w_loaded, 16)
            sp.dma_start(w_v[:, :], io["wv_up"]).then_inc(w_loaded, 16)
            with sp.Fori(0, NB) as tb:
                for n in range(3):
                    for u in range(4):
                        sp.wait_ge(piece_done[n], tb * 4 + u + 1)
                        dst = io["pieces"][u // 2, tb, n, u % 2].rearrange("f h t -> h f t")
                        sp.dma_start(dst, piece[n][:, u, :]).then_inc(piece_sent[n], 16)
            for n in range(3):
                sp.wait_ge(piece_sent[n], 16 * 4 * NB)

        @block.gpsimd
        def _(pool):
            nc.gpsimd.memset(ident[:, :], 0.0).then_inc(ident_ready, 1)
            nc.gpsimd.memset(minus_half[:, :], -0.5).then_inc(const_ready, 1)
            nc.gpsimd.memset(v_all[:, :, :, D:VW], 1.0).then_inc(const_ready, 1)
            nc.gpsimd.memset(keep["mask_row"][:, :], 0.0).then_inc(const_ready, 1)
            nc.gpsimd.memset(keep["ones"][:, :], 1.0).then_inc(const_ready, 1)
            pool.wait_ge(ident_ready, 1)
            nc.gpsimd.affine_select(out=ident[:, :], in_=ident[:, :], compare_op=ALU.not_equal, fill=1.0,
                                    base=0, pattern=[[-1, P]], channel_multiplier=1).then_inc(ident_ready, 1)
            nc.gpsimd.memset(eps[:, :], LN_EPS).then_inc(const_ready, 1)
            pool.wait_ge(const_ready, 5)
            nc.gpsimd.memset(keep["mask_row"][0:1, 0:PAGE], NEG_BIG).then_inc(const_ready, 1)
            nc.gpsimd.memset(keep["mask_row"][0:1, P:P + PAGE], NEG_BIG).then_inc(const_ready, 1)

            def norm(tb):
                pool.wait_ge(mv_done, tb * TPB + TPB)
                nc.gpsimd.tensor_tensor(var[:, :], mv[:, :, 1], eps[:, :], ALU.add).then_inc(var_done, 1)
                pool.wait_ge(var_done, tb + 1)
                nc.gpsimd.tensor_tensor(rstd[:, :], var[:, :], minus_half[:, :], ALU.pow).then_inc(rstd_done, 1)

            def rotate(tb):
                for u in range(4):
                    pool.wait_ge(prod_done, tb * 8 + 2 * u + 2)
                    pool.wait_ge(piece_done[0], tb * 4)
                    pool.wait_ge(rest_done, tb * 4)
                    op = ALU.add if u % 2 else ALU.subtract
                    nc.gpsimd.tensor_tensor(rot[:, u, :], prod_a[:, u, :], prod_b[:, u, :], op).then_inc(rot_done, 1)
                pool.wait_ge(piece_sent[2], tb * 64)
                for u in range(4):
                    pool.wait_ge(rest_done, tb * 4 + u + 1)
                    pool.wait_ge(piece_done[1], tb * 4 + u + 1)
                    nc.gpsimd.tensor_tensor(piece[2][:, u, :], rest[:, u, :], piece[1][:, u, :],
                                            ALU.subtract).then_inc(piece_done[2], 1)

            pool.wait_ge(const_ready, 6)
            norm(0)
            with pool.Fori(0, NB - 1) as tb:
                norm(tb + 1)
                rotate(tb)
            rotate(NB - 1)

        @block.vector
        def _(dve):
            def norm(tb):
                for k in range(TPB):
                    nc.vector.bn_stats(out=stats[:, k, :], in_=x[:, tb * TPB + k, :]).then_inc(stats_done, 1)
                dve.wait_ge(stats_done, tb * TPB + TPB)
                dve.wait_ge(var_done, tb)
                dve.sem_inc(waits_met, 1)
                for k in range(TPB):
                    nc.vector.bn_aggr(out=mv[:, k, :], in_=stats[:, k, :]).then_inc(mv_done, 1)
                dve.wait_ge(rstd_done, tb + 1)
                dve.wait_ge(xt_ready, tb * EC)
                for k in range(TPB):
                    nc.vector.tensor_scalar(xn[:, k, :], x[:, tb * TPB + k, :], mv[:, k, 0:1], rstd[:, k:k + 1],
                                            ALU.subtract, ALU.mult).then_inc(xn_ready, 1)

            def rotate(tb):
                dve.wait_ge(rot_done, tb * 4)
                for s in range(2):
                    dve.wait_ge(qk_ready, tb * 2 + s + 1)
                    even, odd = qk_bank[s]
                    for u, a, b in ((2 * s, cos, sin), (2 * s + 1, sin, cos)):
                        nc.vector.tensor_tensor(prod_a[:, u, :], even, a[:, tb, :], ALU.mult).then_inc(prod_done, 1)
                        nc.vector.tensor_tensor(prod_b[:, u, :], odd, b[:, tb, :], ALU.mult).then_inc(prod_done, 1)
                dve.wait_ge(piece_done[2], tb * 4)
                for u in range(4):
                    dve.wait_ge(piece_done[0], tb * 4 + u + 1)
                    nc.vector.tensor_tensor(rest[:, u, :], rot[:, u, :], piece[0][:, u, :],
                                            ALU.subtract).then_inc(rest_done, 1)

            dve.wait_ge(x_loaded, 16)
            norm(0)
            dve.wait_ge(rope_loaded, 32)
            with dve.Fori(0, NB - 1) as tb:
                norm(tb + 1)
                rotate(tb)
            rotate(NB - 1)

        @block.scalar
        def _(act):
            for name, tile in (("cos", cos), ("sin", sin)):
                table = io[name].rearrange("f (b t) -> f (b t)", t=BLK)
                src = bass.AP(table.tensor, 0, [[0, H], [T, HALF], [1, T]])
                act.dma_start(tile[:, :, :].rearrange("p b t -> p (b t)"), src).then_inc(rope_loaded, 16)

            def project_copies(tb):
                act.wait_ge(qk_ready, tb * 2)
                for c in range(EC):
                    act.wait_ge(xt_ready, tb * EC + c + 1)
                    nc.scalar.activation(xn_t[:, c, :], x_bank[c], ACT.Copy).then_inc(xt_copied, 1)
                act.wait_ge(lat_ready, tb + 1)
                act.wait_ge(v_ready, tb * 2)
                nc.scalar.activation(lat_t[:, :], lat_bank, ACT.Copy).then_inc(lat_copied, 1)
                for k in range(2):
                    act.wait_ge(v_ready, tb * 2 + k + 1)
                    for n in range(2):
                        src = v_bank[k][:, n * E:(n + 1) * E].rearrange("p (h d) -> p h d", h=H)
                        nc.scalar.activation(v_all[:, tb * TPB + 2 * k + n, :, 0:D], src,
                                             ACT.Copy).then_inc(v_copied, 1)

            def cut(tb):
                for n, src, made in ((0, rot, rot_done), (1, rest, rest_done)):
                    act.wait_ge(piece_sent[n], tb * 64)
                    if n:
                        act.wait_ge(piece_done[2], tb * 4)
                    for u in range(4):
                        act.wait_ge(made, tb * 4 + u + 1)
                        nc.scalar.activation(piece[n][:, u, :], src[:, u, :], ACT.Copy).then_inc(piece_done[n], 1)

            act.wait_ge(const_ready, 3)
            project_copies(0)
            with act.Fori(0, NB - 1) as tb:
                project_copies(tb + 1)
                cut(tb)
            cut(NB - 1)

        @block.tensor
        def _(pe):
            pe.wait_ge(ident_ready, 2)
            pe.wait_ge(w_loaded, 64)
            with pe.Fori(0, NB) as tb:
                pe.wait_ge(xn_ready, tb * TPB + TPB)
                pe.wait_ge(xt_copied, tb * EC)
                for c in range(EC):
                    for k in range(TPB):
                        last = nc.tensor.transpose(x_bank[c][:, k * P:(k + 1) * P], xn[:, k, c * P:(c + 1) * P],
                                                   ident[:, :])
                    last.then_inc(xt_ready, 1)
                pe.wait_ge(xt_copied, tb * EC + EC)
                pe.wait_ge(v_copied, tb * TPB)
                for c in range(EC):
                    last = nc.tensor.matmul(lat_bank, w_lat[:, c, :], xn_t[:, c, :], start=c == 0, stop=c == EC - 1)
                last.then_inc(lat_ready, 1)
                pe.wait_ge(lat_copied, tb + 1)
                for k in range(TPB):
                    last = nc.tensor.matmul(v_bank[k // 2][:, (k % 2) * E:(k % 2 + 1) * E],
                                            lat_t[:, k * P:(k + 1) * P], w_v[:, :], start=True, stop=True)
                    if k % 2:
                        last.then_inc(v_ready, 1)
                pe.wait_ge(prod_done, tb * 8)
                for n in range(2):
                    for c in range(EC):
                        last = nc.tensor.matmul(qk_bank[0][n], w_q[:, c, n::2], xn_t[:, c, :],
                                                start=c == 0, stop=c == EC - 1)
                last.then_inc(qk_ready, 1)
                for n in range(2):
                    last = nc.tensor.matmul(qk_bank[1][n], w_k[:, n::2], lat_t[:, :], start=True, stop=True)
                last.then_inc(qk_ready, 1)

TURN_LAG = 3
AHEAD = [(10, 10), (14, 14), (18, 18), (24, 24)]


def max_units(b):
    units = [[(h, r, c, BLK, 0)] for c in range(b) for r in range(TPB) for h in range(G)]
    for r in range(TPB):
        keys = P * (r + 1)
        per = BLK // keys
        per = per if G % per == 0 else 1
        units += [[(h + n, r, b, keys, n * keys) for n in range(per)] for h in range(0, G, per)]
    return units

def attend(nc, ctx, io, keep, psum):
    def sb(name, shape, dt=F32):
        return ctx.enter_context(nc.sbuf_tensor(name, shape, dt))

    def sem(name):
        return ctx.enter_context(nc.semaphore(name))

    ident, v_all, attn = keep["ident"], keep["v_all"], keep["attn"]
    mask_row, ones = keep["mask_row"], keep["ones"]
    q_stack = sb("q_stack", [P, NB, H, BLK], BF16)
    k_stack = sb("k_stack", [P, NB, H, BLK], BF16)
    v_group = sb("v_group", [P, TILES, G, VW])
    probs = sb("probs", [P, 2, G, BLK])
    out_t = sb("out_t", [P, NG, BLK])
    part_max = sb("part_max", [P, G, TPB, NB])
    neg_max = sb("neg_max", [P, G * TPB])
    shift = sb("shift", [G * TPB, SHIFT_ROWS, P], BF16)
    rsum = sb("rsum", [P, TPB, G])

    s_bank = [banks(psum, h) for h in range(G)]
    o_bank = banks(psum, 4)
    m_bank = [banks(psum, n) for n in (5, 6, 7)]

    stack_loaded = [sem(f"stack_loaded{b}") for b in range(NB)]
    one_rows_set = sem("one_rows_set")
    o_cleared = sem("o_cleared")
    m_ready = sem("m_ready")
    m_read = sem("m_read")
    neg_max_done = sem("neg_max_done")
    shift_done = sem("shift_done")
    shift_sent = sem("shift_sent")
    s_ready = sem("s_ready")
    exp_done = sem("exp_done")
    v_staged = sem("v_staged")
    pv_done = sem("pv_done")
    o_copied = sem("o_copied")
    o_turned = sem("o_turned")
    rsum_done = sem("rsum_done")
    out_done = sem("out_done")

    units = [max_units(b) for b in range(NB)]
    steps = [TPB * (b + 1) for b in range(NB)]

    order = [(b, g) for b in range(NB) for g in range(NG)]
    stream = []
    for k, (b, _) in enumerate(order):
        stream += [("unit", k, n) for n in range(len(units[b]))]
        if k:
            stream.insert(len(stream) - len(units[b]) + TURN_LAG, ("turn", k - 1, 0))
    stream.append(("turn", len(order) - 1, 0))

    def cut(k):
        if k + 2 >= len(order):
            return len(stream)
        b, g = order[k + 2]
        return stream.index(("unit", k + 2, 0)) + AHEAD[b][min(g, 1)] + 1

    parts = [stream[:cut(-1)]]
    for k, (b, g) in enumerate(order):
        part = stream[cut(k - 1):cut(k)]
        done = {NG - 2: [k - 2, k - 1] + ([k - 3] if b else []), NG - 1: [k - 1]}.get(g, [])
        for n, kk in enumerate(sorted(done)):
            part.insert(len(part) * (n + 2) // (len(done) + 2), ("out", kk, 0))
        parts.append(part)
    parts.append([("out", len(order) - 1, 0)])
    starts = [sum(len(p) for p in parts[:n]) for n in range(len(parts))]

    part_banks = [[1 if n == len(p) - 1 and n % 3 == 0 else n % 3 for n in range(len(p))] for p in parts]
    bank_of = sum(part_banks, [])

    def since(n, at):
        at += starts[n]
        return next((d for d in range(1, at + 1) if bank_of[at - d] == bank_of[at]), None)

    LOOPED = NG - 2

    def entries_of(b, g):
        static = isinstance(g, int)
        k = b * NG + (g if static else 0)
        for at, (what, kk, n) in enumerate(parts[k + 1]):
            if static:
                yield what, *order[kk], n, starts[k + 1] + at, since(k + 1, at), m_bank[part_banks[k + 1][at]]
            else:
                nearest = min(since(k + 1 + i, at) for i in range(LOOPED))
                yield (what, b, g + (kk - k), n, g * len(parts[k + 1]) + (starts[k + 1] + at), nearest,
                       m_bank[part_banks[k + 1][at]])

    def s_base(b, g):
        return g * steps[b] + NG * sum(steps[:b])

    def index(b, g):
        return g + NG * b

    def first_col(b, s):
        return max(0, s - TPB * b) * P

    def following(b, g):
        if not isinstance(g, int) or g + 1 < NG:
            return b, g + 1
        return (b + 1, 0) if b + 1 < NB else None

    def chunks_before(b, g):
        return g * (b + 1) + NG * sum(range(b + 1))

    def groups(engine, b, body):
        with engine.Fori(0, LOOPED) as g:
            body(b, g)
        for g in range(LOOPED, NG):
            body(b, g)

    with nc.Block() as block:

        @block.sync
        def _(sp):
            def load(b):
                d = [io["pieces"][s, b] for s in range(2)]
                row = H * BLK
                for n, rows in ((0, 3), (1, 2), (2, 1)):
                    at = sum(D * Q_PIECES.count(m) for m in range(n))
                    src = bass.AP(d[0].tensor, d[0].offset + n * D * row, [[0, rows], [row, D], [1, row]])
                    dst = q_stack[at:at + D * rows, b, :, :].rearrange("p h t -> p (h t)")
                    sp.dma_start(dst, src).then_inc(stack_loaded[b], 16)
                for at, rows in ((0, 3), (3, 2), (5, 1)):
                    src = bass.AP(d[1].tensor, d[1].offset, [[row, D * rows], [1, row]])
                    dst = k_stack[D * at:D * (at + rows), b, :, :].rearrange("p h t -> p (h t)")
                    sp.dma_start(dst, src).then_inc(stack_loaded[b], 16)

            def send_shift(b, g):
                sp.wait_ge(shift_done, index(b, g) * 2 + 2)
                for n in range(SHIFT_ROWS):
                    dst = q_stack[TERM_ROWS + n:TERM_ROWS + n + 1, b, bass.ds(g * G, G), :]
                    sp.dma_start(dst, shift[:, n, :]).then_inc(shift_sent, 16)

            load(0)
            for b in range(NB):
                if b + 1 < NB:
                    load(b + 1)
                with sp.Fori(0, NG) as g:
                    send_shift(b, g)
            sp.wait_ge(shift_sent, 16 * SHIFT_ROWS * NG * NB)

        @block.gpsimd
        def _(pool):
            one_bits = 0x3F803F80

            def set_ones(b):
                rows = k_stack[TERM_ROWS:STACK, b, :, :].rearrange("p h t -> p (h t)").bitcast(U32)
                nc.gpsimd.memset(rows, one_bits).then_inc(one_rows_set, 1)

            def stage(b, g, c):
                nc.gpsimd.tensor_copy(v_group[:, c * TPB:(c + 1) * TPB, :, :],
                                      v_all[:, c * TPB:(c + 1) * TPB, bass.ds(g * G, G), :]).then_inc(v_staged, 1)

            set_ones(0)
            for b in range(NB):
                if b + 1 < NB:
                    if b:
                        pool.wait_ge(v_staged, chunks_before(b, 0))
                    set_ones(b + 1)
                pool.wait_ge(one_rows_set, min(b + 2, NB))
                for c in range(b + 1):
                    if 0 < b and c < b:
                        pool.wait_ge(pv_done, s_base(b, 0) - steps[b - 1] + (c + 1) * TPB)
                    stage(b, 0, c)
                with pool.Fori(1, NG) as g:
                    for c in range(b + 1):
                        pool.wait_ge(pv_done, s_base(b, g) + ((c + 1) * TPB - steps[b]))
                        stage(b, g, c)

        @block.vector
        def _(dve):
            nc.vector.memset(o_bank, 0.0).then_inc(o_cleared, 1)

            def maxima(entries):
                for what, b, g, n, at, _, bank in entries:
                    dve.wait_ge(m_ready, at + 1)
                    if what == "unit":
                        if n == 0:
                            dve.wait_ge(neg_max_done, index(b, g))
                        unit = units[b][n]
                        h, r, c, keys, _ = unit[0]
                        m = len(unit)
                        src = bank[:, 0:m * keys].rearrange("p (m k) -> p m k", m=m)
                        nc.vector.tensor_reduce(part_max[:, h:h + m, r, c:c + 1], src, axis=AX_X,
                                                op=ALU.max).then_inc(m_read, 1)
                        if n == len(units[b]) - 1:
                            dve.wait_ge(m_read, at + 1)
                            nc.vector.tensor_reduce(neg_max[:, :], part_max[:, :, :, 0:b + 1], axis=AX_X, op=ALU.max,
                                                    negate=True).then_inc(neg_max_done, 1)
                    elif what == "turn":
                        dve.wait_ge(shift_sent, index(b, g) * 16 * SHIFT_ROWS)
                        rows = bank[0:G * TPB, 0:P]
                        nc.vector.tensor_copy(shift[:, 0, :], rows).then_inc(shift_done, 1)
                        dve.wait_ge(shift_done, index(b, g) * 2 + 1)
                        nc.vector.tensor_tensor(shift[:, 1, :], rows, shift[:, 0, :],
                                                ALU.subtract).then_inc(shift_done, 1)
                        dve.wait_ge(shift_done, index(b, g) * 2 + 2)
                        dve.sem_inc(m_read, 1)
                    else:
                        if index(b, g):
                            dve.wait_ge(out_done, index(b, g))
                        view = bank.rearrange("p (r h w) -> p r h w", r=TPB, h=G)
                        nc.vector.reciprocal(rsum[:, :, :], view[:, :, :, D]).then_inc(rsum_done, 1)
                        dve.wait_ge(rsum_done, index(b, g) + 1)
                        dst = attn[:, TPB * b:TPB * (b + 1), g * G * D:(g + 1) * G * D]
                        nc.vector.tensor_tensor(dst.rearrange("p r (h d) -> p r h d", h=G), view[:, :, :, 0:D],
                                                rsum[:, :, :].unsqueeze(3).to_broadcast([P, TPB, G, D]),
                                                ALU.mult).then_inc(out_done, 1)
                        dve.wait_ge(out_done, index(b, g) + 1)
                        dve.sem_inc(m_read, 1)

            maxima(entries_of(0, -1))
            for b in range(NB):
                groups(dve, b, lambda b, g: maxima(entries_of(b, g)))
            maxima(entries_of(NB, 0))

        @block.scalar
        def _(act):
            def step(b, g, s):
                n = s_base(b, g) + s
                col = first_col(b, s)
                if not isinstance(n, int) or n >= 2:
                    act.wait_ge(pv_done, n - 1)
                for h in range(G):
                    act.wait_ge(s_ready, n * G + h + 1)
                    nc.scalar.activation(probs[:, s % 2, h, col:BLK], s_bank[h][:, col:BLK], ACT.Exp,
                                         scale=ATTN_SCALE).then_inc(exp_done, 1)

            def group(b, g):
                for s in range(1, steps[b]):
                    step(b, g, s)
                if following(b, g):
                    step(*following(b, g), 0)
                act.wait_ge(pv_done, s_base(b, g) + steps[b])
                if b:
                    act.wait_ge(o_turned, index(b, g) - NG + 1)
                nc.scalar.activation(out_t[:, g, :], o_bank, ACT.Copy).then_inc(o_copied, 1)

            step(0, 0, 0)
            for b in range(NB):
                groups(act, b, group)

        @block.tensor
        def _(pe):
            def maxima(entries):
                for what, b, g, n, at, since_last, bank in entries:
                    if since_last is not None:
                        pe.wait_ge(m_read, at + (1 - since_last))
                    if what == "unit":
                        for h, r, c, keys, col in units[b][n]:
                            out = bank[:, col:col + keys]
                            diagonal = c == b
                            last = nc.tensor.matmul(out, q_stack[0:TERM_ROWS, b, g * G + h, r * P:(r + 1) * P],
                                                    k_stack[0:TERM_ROWS, c, g * G + h, 0:keys],
                                                    start=True, stop=not diagonal)
                            if diagonal:
                                last = nc.tensor.matmul(out[:, keys - PAGE:keys], mask_row[0:TERM_ROWS, 0:P],
                                                        ones[0:TERM_ROWS, :], start=False, stop=True)
                        last.then_inc(m_ready, 1)
                    elif what == "turn":
                        pe.wait_ge(neg_max_done, index(b, g) + 1)
                        nc.tensor.transpose(bank[0:G * TPB, 0:P], neg_max[:, :], ident[:, :]).then_inc(m_ready, 1)
                    else:
                        pe.wait_ge(o_copied, index(b, g) + 1)
                        for r in range(TPB):
                            last = nc.tensor.transpose(bank[:, r * P:(r + 1) * P], out_t[:, g, r * P:(r + 1) * P],
                                                       ident[:, :])
                        last.then_inc(m_ready, 1)
                        pe.wait_ge(m_ready, at + 1)
                        pe.sem_inc(o_turned, 1)

            def scores(b, g, s, h):
                n = s_base(b, g) + s
                col = first_col(b, s)
                if not isinstance(n, int) or n:
                    pe.wait_ge(exp_done, (n - 1) * G + h + 1)
                diagonal = s >= TPB * b
                last = nc.tensor.matmul(s_bank[h][:, col:BLK],
                                        k_stack[0:STACK, s // TPB, g * G + h, (s % TPB) * P:(s % TPB + 1) * P],
                                        q_stack[0:STACK, b, g * G + h, col:BLK], start=True, stop=not diagonal)
                if diagonal:
                    last = nc.tensor.matmul(s_bank[h][:, col:col + PAGE], mask_row[0:TERM_ROWS, PAGE:P + PAGE],
                                            ones[0:TERM_ROWS, :], start=False, stop=True)
                last.then_inc(s_ready, 1)

            def weigh(b, g, s):
                n = s_base(b, g) + s
                col = first_col(b, s)
                pe.wait_ge(exp_done, n * G + G)
                if s % TPB == 0:
                    pe.wait_ge(v_staged, chunks_before(b, g) + s // TPB + 1)
                if s == 0:
                    pe.wait_ge(o_copied, index(b, g))
                for h in range(G):
                    last = nc.tensor.matmul(o_bank[32 * h:32 * h + VW, col:BLK], v_group[:, s, h, :],
                                            probs[:, s % 2, h, col:BLK], start=s == 0, stop=s == steps[b] - 1)
                last.then_inc(pv_done, 1)

            def group(b, g):
                entries = list(entries_of(b, g))
                pairs = [((b, g), s) for s in range(1, steps[b])]
                if following(b, g):
                    pairs.append((following(b, g), 0))
                weights = [BLK - first_col(where[0], s) for where, s in pairs]
                done = 0
                for i, (where, s) in enumerate(pairs):
                    if s == 0:
                        due = max([done] + [n + 1 for n, e in enumerate(entries) if e[0] == "turn"])
                        maxima(entries[done:due])
                        done = due
                        pe.wait_ge(shift_sent, (index(*where) + 1) * 16 * SHIFT_ROWS)
                    for h in range(G):
                        scores(*where, s, h)
                        due = len(entries) * (sum(weights[:i]) + weights[i] * (h + 1) / (G + 1)) // sum(weights)
                        maxima(entries[done:int(due)])
                        done = max(done, int(due))
                    weigh(b, g, s - 1 if s else steps[b] - 1)
                    due = len(entries) * sum(weights[:i + 1]) // sum(weights)
                    maxima(entries[done:due])
                    done = max(done, due)
                if not following(b, g):
                    weigh(b, g, steps[b] - 1)

            pe.wait_ge(o_cleared, 1)
            pe.wait_ge(stack_loaded[0], 96)
            maxima(entries_of(0, -1))
            pe.wait_ge(one_rows_set, 1)
            pe.wait_ge(shift_sent, 16 * SHIFT_ROWS)
            for h in range(G):
                scores(0, 0, 0, h)
            for b in range(NB):
                if b + 1 < NB:
                    pe.wait_ge(one_rows_set, b + 2)
                    pe.wait_ge(stack_loaded[b + 1], 96)
                groups(pe, b, group)
            maxima(entries_of(NB, 0))

def fold(nc, ctx, io, keep, psum):
    def sb(name, shape, dt=F32):
        return ctx.enter_context(nc.sbuf_tensor(name, shape, dt))

    def sem(name):
        return ctx.enter_context(nc.semaphore(name))

    x, attn, ident = keep["x"], keep["attn"], keep["ident"]
    ctx_t, w_qk, bias_c, v_out = keep["ctx_t"], keep["w_qk"], keep["bias_c"], keep["v_out"]
    x2_t, row_fill, w_tern = keep["x2_t"], keep["row_fill"], keep["w_tern"]
    wo = sb("wo", [P, EC, E])
    cw_q = sb("cw_q", [P, HC, E + 1])
    cw_k = sb("cw_k", [P, HC, E])
    cw_v = sb("cw_v", [P, HC, E])
    cw_o = sb("cw_o", [P, HC, E])
    b_k = sb("b_k", [P, HC])
    b_v = sb("b_v", [P, HC])
    b_o = sb("b_o", [P, E])
    w_vo = sb("w_vo", [P, EC, E])
    row_w = sb("row_w", [P, E + 1])
    row_b = sb("row_b", [P, E])
    ffn_w = sb("ffn_w", [P, EC, E])
    abs_sum = sb("abs_sum", [P, 1])
    abs_all = sb("abs_all", [P, 1])
    limit = sb("limit", [P, 2])
    above = sb("above", [P, EC, E])
    attn_s = sb("attn_s", [P, TPB, E])
    attn_t = sb("attn_t", [P, EC, BLK])
    stats = sb("stats2", [P, TPB, 6])
    mv = sb("mv2", [P, TPB, 2])
    var = sb("var2", [P, TPB])
    rstd = sb("rstd2", [P, TPB])
    eps = sb("eps2", [P, TPB])
    minus_half = sb("minus_half2", [P, TPB])
    xn = sb("xn2", [P, TPB, E])
    dump = sb("dump", [P, E])
    dots = sb("dots", [P, TPB])

    a_bank = [banks(psum, 0), banks(psum, 1)]
    y_bank = [banks(psum, 2), banks(psum, 3)]
    n_bank = [banks(psum, 4), banks(psum, 5)]
    w_bank = [banks(psum, 6), banks(psum, 7)]

    att_w_loaded = sem("att_w_loaded")
    cross_w_loaded = sem("cross_w_loaded")
    ctx_loaded = sem("ctx_loaded")
    ffn_w_loaded = sem("ffn_w_loaded")
    set_done = sem("set_done")
    staged = sem("staged")
    a_ready = sem("a_ready")
    a_copied = sem("a_copied")
    y_ready = sem("y_ready")
    x_added = sem("x_added")
    stats_done = sem("stats_done2")
    waits_met = sem("waits_met2")
    mv_done = sem("mv_done2")
    var_done = sem("var_done2")
    rstd_done = sem("rstd_done2")
    xn_ready = sem("xn_ready2")
    dot_done = sem("dot_done")
    fill_done = sem("fill_done")
    bias_added = sem("bias_added")
    n_ready = sem("n_ready")
    n_copied = sem("n_copied")
    w_ready = sem("w_ready")
    w_copied = sem("w_copied")
    row_done = sem("row_done")
    tern_step = sem("tern_step")
    abs_ready = sem("abs_ready")
    abs_everywhere = sem("abs_everywhere")
    limit_done = sem("limit_done")

    V_FIRST = 7
    V_PAIRS = -(-S2_TILES // 2)
    N_W = V_FIRST + V_PAIRS

    with nc.Block() as block:

        @block.sync
        def _(sp):
            sp.dma_start(wo[:, :, :], io["wo"].rearrange("(c p) e -> p c e", p=P)).then_inc(att_w_loaded, 16)
            sp.dma_start(cw_q[:, :, 0:E], io["Wq"].rearrange("(c p) e -> p c e", p=P)).then_inc(cross_w_loaded, 16)
            sp.dma_start(cw_k[:, :, :], io["Wk"].rearrange("(c p) e -> p c e", p=P)).then_inc(cross_w_loaded, 16)
            sp.dma_start(cw_v[:, :, :], io["Wv"].rearrange("(c p) e -> p c e", p=P)).then_inc(cross_w_loaded, 16)
            sp.dma_start(cw_o[:, :, :], io["WoT"].rearrange("(c p) e -> p c e", p=P)).then_inc(cross_w_loaded, 16)
            with nc.allow_non_contiguous_dma(reason="bias vectors by partition"):
                sp.dma_start(cw_q[:, :, E:E + 1], io["bq"].rearrange("(c p o) -> p c o", p=P, o=1)).then_inc(cross_w_loaded, 16)
                sp.dma_start(b_k[:, :], io["bk"].rearrange("(c p) -> p c", p=P)).then_inc(cross_w_loaded, 16)
                sp.dma_start(b_v[:, :], io["bv"].rearrange("(c p) -> p c", p=P)).then_inc(cross_w_loaded, 16)
            sp.dma_start(b_o[:, :], bass.AP(io["bo"].tensor, 0, [[0, P], [1, E]])).then_inc(cross_w_loaded, 16)
            sp.dma_start(ctx_t[:, :, :], io["ctxT"].rearrange("(c p) s -> p c s", p=P)).then_inc(ctx_loaded, 16)
            sp.dma_start(ffn_w[:, :, :], io["ffn_w"].rearrange("(c p) e -> p c e", p=P)).then_inc(ffn_w_loaded, 16)

        @block.gpsimd
        def _(pool):
            nc.gpsimd.memset(eps[:, :], LN_EPS).then_inc(set_done, 1)
            nc.gpsimd.memset(minus_half[:, :], -0.5).then_inc(set_done, 1)
            pool.wait_ge(set_done, 2)

            def stage(tb):
                pool.wait_ge(a_ready, tb * EC)
                nc.gpsimd.tensor_copy(attn_s[:, :, :], attn[:, bass.ds(tb * TPB, TPB), :]).then_inc(staged, 1)

            def norm(tb):
                pool.wait_ge(mv_done, tb * TPB + TPB)
                nc.gpsimd.tensor_tensor(var[:, :], mv[:, :, 1], eps[:, :], ALU.add).then_inc(var_done, 1)
                pool.wait_ge(var_done, tb + 1)
                nc.gpsimd.tensor_tensor(rstd[:, :], var[:, :], minus_half[:, :], ALU.pow).then_inc(rstd_done, 1)
                pool.wait_ge(row_done, 2)
                pool.wait_ge(xn_ready, tb * TPB + TPB)
                tiles = x[:, bass.ds(tb * TPB, TPB), :]
                bias = row_b[:, :].unsqueeze(1).to_broadcast([P, TPB, E])
                nc.gpsimd.tensor_tensor(tiles, tiles, bias, ALU.add).then_inc(bias_added, 1)

            stage(0)
            with pool.Fori(0, NB - 1) as tb:
                stage(tb + 1)
                norm(tb)
            norm(NB - 1)
            pool.wait_ge(abs_ready, 1)
            nc.gpsimd.partition_all_reduce(abs_all[:, :], abs_sum[:, :], P, ReduceOp.add).then_inc(abs_everywhere, 1)

        @block.vector
        def _(dve):
            def rows():
                dve.wait_ge(w_ready, 5)
                nc.vector.tensor_copy(row_w[:, :], w_bank[0][:, 0:E + 1]).then_inc(row_done, 1)
                dve.wait_ge(w_ready, 6)
                dve.wait_ge(cross_w_loaded, 16 * 8)
                nc.vector.tensor_tensor(row_b[:, :], w_bank[1][:, 0:E], b_o[:, :], ALU.add).then_inc(row_done, 1)

            def block_of_tiles(tb):
                for k in range(2):
                    dve.wait_ge(y_ready, tb * 2 + k + 1)
                    tiles = x[:, bass.ds(tb * TPB + 2 * k, 2), :]
                    nc.vector.tensor_tensor(tiles, y_bank[k].rearrange("p (t e) -> p t e", t=2), tiles,
                                            ALU.add).then_inc(x_added, 1)
                dve.wait_ge(x_added, tb * 2 + 2)
                dve.sem_inc(waits_met, 1)
                for k in range(TPB):
                    nc.vector.bn_stats(out=stats[:, k, :], in_=x[:, tb * TPB + k, :]).then_inc(stats_done, 1)
                dve.wait_ge(stats_done, tb * TPB + TPB)
                dve.wait_ge(var_done, tb)
                dve.sem_inc(waits_met, 1)
                for k in range(TPB):
                    nc.vector.bn_aggr(out=mv[:, k, :], in_=stats[:, k, :]).then_inc(mv_done, 1)
                dve.wait_ge(rstd_done, tb + 1)
                dve.wait_ge(n_ready, tb * EC)
                for k in range(TPB):
                    nc.vector.tensor_scalar(xn[:, k, :], x[:, tb * TPB + k, :], mv[:, k, 0:1], rstd[:, k:k + 1],
                                            ALU.subtract, ALU.mult).then_inc(xn_ready, 1)
                for k in range(TPB):
                    dve.wait_ge(xn_ready, tb * TPB + k + 1)
                    dve.wait_ge(dot_done, tb * TPB + k)
                    nc.vector.tensor_tensor_reduce(out=dump[:, :], in0=xn[:, k, :], in1=row_w[:, 0:E], scale=1.0,
                                                   scalar=row_w[:, E:E + 1], op0=ALU.mult, op1=ALU.add,
                                                   accum_out=dots[:, k:k + 1]).then_inc(dot_done, 1)
                dve.wait_ge(dot_done, tb * TPB + TPB)
                nc.vector.tensor_scalar(row_fill[:, bass.ds(tb * TPB, TPB)], dots[:, :], -1.0, X_FILL,
                                        ALU.mult, ALU.add).then_inc(fill_done, 1)

            rows()
            dve.wait_ge(row_done, 2)
            with dve.Fori(0, NB) as tb:
                block_of_tiles(tb)
            dve.wait_ge(ffn_w_loaded, 16)
            nc.vector.tensor_reduce(abs_sum[:, :], ffn_w[:, :, :], axis=mybir.AxisListType.XY, op=ALU.add,
                                    apply_absolute_value=True).then_inc(abs_ready, 1)
            dve.wait_ge(abs_everywhere, 1)
            nc.vector.tensor_scalar(keep["beta"][:, :], abs_all[:, :], 1.0 / (E * E), None, ALU.mult).then_inc(limit_done, 1)
            dve.wait_ge(limit_done, 1)
            nc.vector.tensor_scalar(limit[:, 0:1], keep["beta"][:, :], FFN_EPS, 0.5, ALU.add, ALU.mult).then_inc(limit_done, 1)
            nc.vector.tensor_scalar(limit[:, 1:2], keep["beta"][:, :], FFN_EPS, -0.5, ALU.add, ALU.mult).then_inc(limit_done, 1)
            dve.wait_ge(limit_done, 3)
            nc.vector.tensor_scalar(above[:, :, :], ffn_w[:, :, :], limit[:, 0:1], None, ALU.is_gt).then_inc(tern_step, 1)
            nc.vector.tensor_scalar(ffn_w[:, :, :], ffn_w[:, :, :], limit[:, 1:2], None, ALU.is_lt).then_inc(tern_step, 1)
            dve.wait_ge(tern_step, 2)
            nc.vector.tensor_tensor(w_tern[:, :, :], above[:, :, :], ffn_w[:, :, :], ALU.subtract).then_inc(tern_step, 1)

        @block.scalar
        def _(act):
            def out(n, dst, src):
                act.wait_ge(w_ready, n + 1)
                nc.scalar.activation(dst, src, ACT.Copy).then_inc(w_copied, 1)

            for c in range(EC):
                out(c, w_qk[:, c, :], w_bank[c % 2][:, 0:E])
            for c in range(EC):
                out(2 + c, w_vo[:, c, :], w_bank[c % 2][:, 0:E])
            act.wait_ge(row_done, 2)
            out(6, bias_c[:, :], w_bank[0][:, 0:EC])
            for n in range(V_PAIRS):
                src = w_bank[(V_FIRST + n) % 2]
                for m in range(2):
                    j = 2 * n + m
                    if j < S2_TILES:
                        rows = P if j < S2_TILES - 1 else S2_TAIL
                        act.wait_ge(w_ready, V_FIRST + n + 1)
                        done = nc.scalar.activation(v_out[0:rows, j, :], src[0:rows, m * E:(m + 1) * E], ACT.Copy)
                done.then_inc(w_copied, 1)

            def turn_attn(tb):
                act.wait_ge(y_ready, tb * 2)
                for c in range(EC):
                    act.wait_ge(a_ready, tb * EC + c + 1)
                    nc.scalar.activation(attn_t[:, c, :], a_bank[c], ACT.Copy).then_inc(a_copied, 1)

            def turn_norm(tb):
                for c in range(EC):
                    act.wait_ge(n_ready, tb * EC + c + 1)
                    nc.scalar.activation(x2_t[:, c, tb, :], n_bank[c], ACT.Copy).then_inc(n_copied, 1)

            turn_attn(0)
            with act.Fori(0, NB - 1) as tb:
                turn_attn(tb + 1)
                turn_norm(tb)
            turn_norm(NB - 1)

        @block.tensor
        def _(pe):
            pe.wait_ge(cross_w_loaded, 16 * 8)
            for c in range(EC):
                for e in range(HC):
                    last = nc.tensor.matmul(w_bank[c][:, 0:E], cw_q[:, e, c * P:(c + 1) * P], cw_k[:, e, :],
                                            start=e == 0, stop=e == HC - 1)
                last.then_inc(w_ready, 1)
            for c in range(EC):
                pe.wait_ge(w_copied, c + 1)
                for e in range(HC):
                    last = nc.tensor.matmul(w_bank[c][:, 0:E], cw_v[:, e, c * P:(c + 1) * P], cw_o[:, e, :],
                                            start=e == 0, stop=e == HC - 1)
                last.then_inc(w_ready, 1)
            pe.wait_ge(w_copied, 3)
            for e in range(HC):
                last = nc.tensor.matmul(w_bank[0][:, 0:E + 1], b_k[:, e:e + 1].to_broadcast([P, P]), cw_q[:, e, :],
                                        start=e == 0, stop=e == HC - 1)
            last.then_inc(w_ready, 1)
            pe.wait_ge(w_copied, 4)
            for e in range(HC):
                last = nc.tensor.matmul(w_bank[1][:, 0:E], b_v[:, e:e + 1].to_broadcast([P, P]), cw_o[:, e, :],
                                        start=e == 0, stop=e == HC - 1)
            last.then_inc(w_ready, 1)
            pe.wait_ge(row_done, 1)
            for c in range(EC):
                for e in range(HC):
                    last = nc.tensor.matmul(w_bank[0][:, c:c + 1], cw_k[:, e, c * P:(c + 1) * P], cw_q[:, e, E:E + 1],
                                            start=e == 0, stop=e == HC - 1)
            last.then_inc(w_ready, 1)
            pe.wait_ge(ctx_loaded, 16)
            for n in range(V_PAIRS):
                pe.wait_ge(row_done, 2)
                if n >= 1:
                    pe.wait_ge(w_copied, n + 4)
                for j in range(2 * n, min(2 * n + 2, S2_TILES)):
                    keys = P if j < S2_TILES - 1 else S2_TAIL
                    dst = w_bank[(V_FIRST + n) % 2][0:keys, (j % 2) * E:(j % 2 + 1) * E]
                    for c in range(EC):
                        last = nc.tensor.matmul(dst, ctx_t[:, c, j * P:j * P + keys], w_vo[:, c, :],
                                                start=c == 0, stop=c == EC - 1)
                last.then_inc(w_ready, 1)
            pe.wait_ge(att_w_loaded, 16)

            def output(tb):
                pe.wait_ge(staged, tb + 1)
                pe.wait_ge(a_copied, tb * EC)
                for c in range(EC):
                    for k in range(TPB):
                        last = nc.tensor.transpose(a_bank[c][:, k * P:(k + 1) * P], attn_s[:, k, c * P:(c + 1) * P],
                                                   ident[:, :])
                    last.then_inc(a_ready, 1)
                pe.wait_ge(a_copied, tb * EC + EC)
                pe.wait_ge(x_added, tb * 2)
                for k in range(TPB):
                    for c in range(EC):
                        last = nc.tensor.matmul(y_bank[k // 2][:, (k % 2) * E:(k % 2 + 1) * E],
                                                attn_t[:, c, k * P:(k + 1) * P], wo[:, c, :],
                                                start=c == 0, stop=c == EC - 1)
                    if k % 2:
                        last.then_inc(y_ready, 1)

            def normed(tb):
                pe.wait_ge(xn_ready, tb * TPB + TPB)
                pe.wait_ge(n_copied, tb * EC)
                for c in range(EC):
                    for k in range(TPB):
                        last = nc.tensor.transpose(n_bank[c][:, k * P:(k + 1) * P], xn[:, k, c * P:(c + 1) * P],
                                                   ident[:, :])
                    last.then_inc(n_ready, 1)

            output(0)
            with pe.Fori(0, NB - 1) as tb:
                output(tb + 1)
                normed(tb)
            normed(NB - 1)

def cross(nc, ctx, io, keep, psum):
    def sb(name, shape, dt=F32):
        return ctx.enter_context(nc.sbuf_tensor(name, shape, dt))

    def sem(name):
        return ctx.enter_context(nc.semaphore(name))

    x, ident = keep["x"], keep["ident"]
    ctx_t, w_qk, bias_c, v_out = keep["ctx_t"], keep["w_qk"], keep["bias_c"], keep["v_out"]
    x2_t, row_fill, x3, abs_max = keep["x2_t"], keep["row_fill"], keep["x3"], keep["abs_max"]
    mask = sb("mask", [P, 2, S2], I32)
    zeros = sb("zeros_s2", [P, S2])
    qc_t = sb("qc_t", [P, 2, EC, P])
    e = sb("e", [P, 2, S2])
    neg = sb("neg", [P, 2])
    esum = sb("esum", [P, 2])
    rsum = sb("rsum_x", [P, 2])
    p_t = sb("p_t", [P, S2_TILES, P])
    gamma = sb("gamma", [P, E])
    beta = sb("beta_row", [P, E])
    stats = sb("stats3", [P, 6])
    mv = sb("mv3", [P, 2])
    va = sb("va", [P, 1])
    ra = sb("ra", [P, 1])
    rr = sb("rr", [P, 1])
    vb = sb("vb", [P, 1])
    vc = sb("vc", [P, 1])
    rb = sb("rb", [P, 1])
    scale = sb("scale3", [P, 1])
    consts = sb("consts3", [P, 3])
    z = sb("z", [P, E])
    zg = sb("zg", [P, E])

    CHUNKS = [(c * TPB, min(TPB, S2_TILES - c * TPB)) for c in range(-(-S2_TILES // TPB))]
    NCH = len(CHUNKS)
    e_bank = psum[:, 0:S2]
    t_bank = [banks(psum, 4), banks(psum, 5)]
    y_bank = banks(psum, 6)
    q_bank = banks(psum, 7)

    mask_loaded = [sem(f"mask_loaded{n}") for n in range(2)]
    rows_loaded = sem("rows_loaded")
    set_done = sem("set_done3")
    qc_ready = sem("qc_ready")
    qc_copied = sem("qc_copied")
    filled = sem("filled")
    e_ready = sem("e_ready")
    e_taken = sem("e_taken")
    max_done = sem("max_done")
    exp_done = sem("exp_done3")
    t_ready = sem("t_ready3")
    t_copied_a = sem("t_copied_a")
    t_copied_v = sem("t_copied_v")
    y_ready = sem("y_ready3")
    rsum_done = sem("rsum_done3")
    x_added = sem("x_added3")
    stats_done = sem("stats_done3")
    mv_done = sem("mv_done3")
    pool_step = sem("pool_step")
    z_done = sem("z_done")
    zg_done = sem("zg_done")
    xn3_done = sem("xn3_done")
    abs_done = sem("abs_done")
    waits_met = sem("waits_met3")
    POOL_STEPS = 7

    PAIRS = TILES // 2

    def pairs(engine, body, first=None):
        with engine.Fori(0, PAIRS - 1) as k:
            for h in range(2):
                body(2 * k + h, h, False)
        for h in range(2):
            body(2 * (PAIRS - 1) + h, h, h == 1)

    with nc.Block() as block:

        @block.sync
        def _(sp):
            sp.dma_start(gamma[:, :], bass.AP(io["gamma"].tensor, 0, [[0, P], [1, E]])).then_inc(rows_loaded, 16)
            sp.dma_start(beta[:, :], bass.AP(io["beta"].tensor, 0, [[0, P], [1, E]])).then_inc(rows_loaded, 16)
            masks = io["mask"].rearrange("(t p) s -> t p s", p=P)
            for h in range(2):
                sp.dma_start(mask[:, h, :], masks[h]).then_inc(mask_loaded[h], 16)
            with sp.Fori(0, PAIRS - 1) as k:
                for h in range(2):
                    sp.wait_ge(e_taken, 2 * k + h + 1)
                    sp.dma_start(mask[:, h, :], masks[2 * k + (h + 2)]).then_inc(mask_loaded[h], 16)

        @block.gpsimd
        def _(pool):
            nc.gpsimd.memset(zeros[:, :], 0.0).then_inc(set_done, 1)
            for n, value in enumerate((LN_EPS, FFN_LN_EPS, -0.5)):
                nc.gpsimd.memset(consts[:, n:n + 1], value).then_inc(set_done, 1)
            pool.wait_ge(set_done, 4)

            def body(i, h, last):
                if not last:
                    pool.wait_ge(t_ready, i * NCH)
                    nc.gpsimd.tensor_tensor(e[:, 1 - h, :], zeros[:, :],
                                            row_fill[:, bass.ds(i + 1, 1)].to_broadcast([P, S2]),
                                            ALU.add).then_inc(filled, 1)
                pool.wait_ge(mv_done, i + 1)
                n = i * POOL_STEPS
                nc.gpsimd.tensor_tensor(va[:, :], mv[:, 1:2], consts[:, 0:1], ALU.add).then_inc(pool_step, 1)
                pool.wait_ge(pool_step, n + 1)
                nc.gpsimd.tensor_tensor(ra[:, :], va[:, :], consts[:, 2:3], ALU.pow).then_inc(pool_step, 1)
                pool.wait_ge(pool_step, n + 2)
                nc.gpsimd.tensor_tensor(rr[:, :], ra[:, :], ra[:, :], ALU.mult).then_inc(pool_step, 1)
                pool.wait_ge(pool_step, n + 3)
                nc.gpsimd.tensor_tensor(vb[:, :], rr[:, :], mv[:, 1:2], ALU.mult).then_inc(pool_step, 1)
                pool.wait_ge(pool_step, n + 4)
                nc.gpsimd.tensor_tensor(vc[:, :], vb[:, :], consts[:, 1:2], ALU.add).then_inc(pool_step, 1)
                pool.wait_ge(pool_step, n + 5)
                nc.gpsimd.tensor_tensor(rb[:, :], vc[:, :], consts[:, 2:3], ALU.pow).then_inc(pool_step, 1)
                pool.wait_ge(pool_step, n + 6)
                nc.gpsimd.tensor_tensor(scale[:, :], ra[:, :], rb[:, :], ALU.mult).then_inc(pool_step, 1)
                pool.wait_ge(xn3_done, i)
                pool.wait_ge(z_done, i + 1)
                nc.gpsimd.tensor_tensor(zg[:, :], z[:, :], gamma[:, :], ALU.mult).then_inc(zg_done, 1)
                pool.wait_ge(zg_done, i + 1)
                nc.gpsimd.tensor_tensor(x3[:, bass.ds(i, 1), :].rearrange("p o e -> p (o e)"), zg[:, :], beta[:, :], ALU.add).then_inc(xn3_done, 1)

            pool.wait_ge(rows_loaded, 32)
            nc.gpsimd.tensor_tensor(e[:, 0, :], zeros[:, :], row_fill[:, 0:1].to_broadcast([P, S2]),
                                    ALU.add).then_inc(filled, 1)
            pool.wait_ge(filled, 1)
            pairs(pool, body)

        @block.vector
        def _(dve):
            def take(i, h):
                dve.wait_ge(mask_loaded[h], (i - h) * 8 + 16)
                dve.wait_ge(filled, i + 1)
                dve.wait_ge(e_ready, i + 1)
                dve.sem_inc(waits_met, 1)
                nc.vector.copy_predicated(e[:, h, :], mask[:, h, :], e_bank).then_inc(e_taken, 1)
                dve.wait_ge(e_taken, i + 1)
                nc.vector.tensor_reduce(neg[:, h:h + 1], e[:, h, :], axis=AX_X, op=ALU.max).then_inc(max_done, 1)
                dve.wait_ge(max_done, 2 * i + 1)
                nc.vector.tensor_scalar(neg[:, h:h + 1], neg[:, h:h + 1], -X_SCALE, None,
                                        ALU.mult).then_inc(max_done, 1)

            def body(i, h, last):
                for n, (j, m) in enumerate(CHUNKS):
                    if n % 2:
                        rows = P if n < NCH - 1 else S2_TAIL
                        dve.wait_ge(y_ready, i)
                        dve.wait_ge(t_ready, i * NCH + n + 1)
                        nc.vector.tensor_copy(p_t[0:rows, j:j + m, :].rearrange("p j q -> p (j q)"),
                                              t_bank[1][0:rows, 0:m * P]).then_inc(t_copied_v, 1)
                if not last:
                    take(i + 1, 1 - h)
                dve.wait_ge(exp_done, i + 1)
                nc.vector.reciprocal(rsum[:, h:h + 1], esum[:, h:h + 1]).then_inc(rsum_done, 1)
                dve.wait_ge(rsum_done, i + 1)
                dve.wait_ge(y_ready, i + 1)
                nc.vector.scalar_tensor_tensor(out=x[:, i, :], in0=y_bank[:, 0:E], scalar=rsum[:, h:h + 1],
                                               in1=x[:, i, :], op0=ALU.mult, op1=ALU.add).then_inc(x_added, 1)
                dve.wait_ge(x_added, i + 1)
                dve.sem_inc(waits_met, 1)
                nc.vector.bn_stats(out=stats[:, :], in_=x[:, i, :]).then_inc(stats_done, 1)
                dve.wait_ge(stats_done, i + 1)
                dve.wait_ge(pool_step, i * POOL_STEPS)
                dve.sem_inc(waits_met, 1)
                nc.vector.bn_aggr(out=mv[:, :], in_=stats[:, :]).then_inc(mv_done, 1)
                dve.wait_ge(pool_step, i * POOL_STEPS + POOL_STEPS)
                dve.wait_ge(zg_done, i)
                nc.vector.tensor_scalar(z[:, :], x[:, i, :], mv[:, 0:1], scale[:, :],
                                        ALU.subtract, ALU.mult).then_inc(z_done, 1)
                dve.wait_ge(xn3_done, i + 1)
                nc.vector.tensor_reduce(abs_max[:, bass.ds(i, 1)], x3[:, i, :], axis=AX_X, op=ALU.max,
                                        apply_absolute_value=True).then_inc(abs_done, 1)

            take(0, 0)
            pairs(dve, body)

        @block.scalar
        def _(act):
            def prepare(i, h):
                act.wait_ge(qc_ready, i + 1)
                for c in range(EC):
                    nc.scalar.activation(qc_t[:, h, c, :], q_bank[:, c * P:(c + 1) * P], ACT.Identity,
                                         bias=bias_c[:, c:c + 1]).then_inc(qc_copied, 1)

            def exponential(i, h):
                act.wait_ge(max_done, 2 * i + 2)
                nc.scalar.activation(e[:, h, :], e[:, h, :], ACT.Exp, scale=X_SCALE, bias=neg[:, h:h + 1],
                                     accum_out=esum[:, h:h + 1]).then_inc(exp_done, 1)

            def body(i, h, last):
                if not last:
                    prepare(i + 1, 1 - h)
                for n, (j, m) in enumerate(CHUNKS):
                    if n % 2 == 0:
                        act.wait_ge(y_ready, i)
                        act.wait_ge(t_ready, i * NCH + n + 1)
                        nc.scalar.activation(p_t[:, j:j + m, :].rearrange("p j q -> p (j q)"),
                                             t_bank[0][:, 0:m * P], ACT.Copy).then_inc(t_copied_a, 1)
                if not last:
                    act.wait_ge(rsum_done, i)
                    exponential(i + 1, 1 - h)

            prepare(0, 0)
            exponential(0, 0)
            pairs(act, body)

        @block.tensor
        def _(pe):
            def score(i, h):
                pe.wait_ge(qc_copied, i * EC)
                for c in range(EC):
                    for k in range(EC):
                        last = nc.tensor.matmul(q_bank[:, c * P:(c + 1) * P], w_qk[:, k, c * P:(c + 1) * P],
                                                x2_t[:, k, :, :].rearrange("p b t -> p (b t)")[:, bass.ds(i * P, P)],
                                                start=k == 0, stop=k == EC - 1)
                last.then_inc(qc_ready, 1)
                pe.wait_ge(e_taken, i)
                pe.wait_ge(qc_copied, (i + 1) * EC)
                for c0 in range(0, S2, BLK):
                    c1 = min(c0 + BLK, S2)
                    for k in range(EC):
                        last = nc.tensor.matmul(e_bank[:, c0:c1], qc_t[:, h, k, :], ctx_t[:, k, c0:c1],
                                                start=k == 0, stop=k == EC - 1)
                last.then_inc(e_ready, 1)

            def body(i, h, last):
                if not last:
                    score(i + 1, 1 - h)
                pe.wait_ge(exp_done, i + 1)
                for n, (j0, m) in enumerate(CHUNKS):
                    if n >= 2:
                        if n % 2:
                            pe.wait_ge(t_copied_v, i * (NCH // 2) + n // 2)
                        else:
                            pe.wait_ge(t_copied_a, i * (NCH - NCH // 2) + n // 2)
                    for j in range(j0, j0 + m):
                        keys = P if j < S2_TILES - 1 else S2_TAIL
                        last_t = nc.tensor.transpose(t_bank[n % 2][0:keys, (j - j0) * P:(j - j0 + 1) * P],
                                                     e[:, h, j * P:j * P + keys], ident[:, :])
                    last_t.then_inc(t_ready, 1)
                pe.wait_ge(x_added, i)
                for n, (j0, m) in enumerate(CHUNKS):
                    if n % 2:
                        pe.wait_ge(t_copied_v, i * (NCH // 2) + n // 2 + 1)
                    else:
                        pe.wait_ge(t_copied_a, i * (NCH - NCH // 2) + n // 2 + 1)
                    for j in range(j0, j0 + m):
                        keys = P if j < S2_TILES - 1 else S2_TAIL
                        mm = nc.tensor.matmul(y_bank[:, 0:E], p_t[0:keys, j, :], v_out[0:keys, j, :],
                                              start=j == 0, stop=j == S2_TILES - 1)
                mm.then_inc(y_ready, 1)

            score(0, 0)
            pairs(pe, body)

def feed(nc, ctx, io, keep, psum):
    def sb(name, shape, dt=F32):
        return ctx.enter_context(nc.sbuf_tensor(name, shape, dt))

    def sem(name):
        return ctx.enter_context(nc.semaphore(name))

    x, x3, ident, w_tern = keep["x"], keep["x3"], keep["ident"], keep["w_tern"]
    top = sb("top", [P, 1])
    top_all = sb("top_all", [P, 1])
    to_q = sb("to_q", [P, 1])
    back_1 = sb("back_1", [P, 1])
    back = sb("back", [P, 1])
    scaled = sb("scaled", [P, TPB, E])
    xq = sb("xq", [P, TPB, E])
    xq_t = sb("xq_t", [P, EC, BLK])
    y = sb("y", [P, 2, TPB, E])

    x_bank = [banks(psum, 0), banks(psum, 1)]
    y_bank = [banks(psum, 2), banks(psum, 3)]

    top_done = sem("top_done")
    top_everywhere = sem("top_everywhere")
    factor_done = sem("factor_done")
    scaled_done = sem("scaled_done")
    xq_done = sem("xq_done")
    xt_ready = sem("xt_ready4")
    xt_copied = sem("xt_copied4")
    y_ready = sem("y_ready4")
    y_added = sem("y_added")
    y_sent = [sem(f"y_sent{n}") for n in range(2)]

    with nc.Block() as block:

        @block.sync
        def _(sp):
            out = io["out"].rearrange("(b t p) e -> b p t e", p=P, t=TPB)
            for tb in range(NB):
                sp.wait_ge(y_added, tb * TPB + TPB)
                sp.dma_start(out[tb], y[:, tb % 2, :, :]).then_inc(y_sent[tb % 2], 16)
            for n in range(2):
                sp.wait_ge(y_sent[n], 16 * NB // 2)

        @block.gpsimd
        def _(pool):
            pool.wait_ge(top_done, 1)
            nc.gpsimd.partition_all_reduce(top_all[:, :], top[:, :], P, ReduceOp.max).then_inc(top_everywhere, 1)

        @block.vector
        def _(dve):
            nc.vector.tensor_reduce(top[:, :], keep["abs_max"][:, :], axis=AX_X, op=ALU.max).then_inc(top_done, 1)
            dve.wait_ge(top_everywhere, 1)
            nc.vector.reciprocal(to_q[:, :], top_all[:, :]).then_inc(factor_done, 1)
            nc.vector.tensor_tensor(back_1[:, :], top_all[:, :], keep["beta"][:, :], ALU.mult).then_inc(factor_done, 1)
            dve.wait_ge(factor_done, 2)
            nc.vector.tensor_scalar(to_q[:, :], to_q[:, :], QB, None, ALU.mult).then_inc(factor_done, 1)
            nc.vector.tensor_scalar(back[:, :], back_1[:, :], 1.0 / QB, None, ALU.mult).then_inc(factor_done, 1)
            dve.wait_ge(factor_done, 4)

            def clip(tb):
                dve.wait_ge(xt_ready, tb * EC)
                dve.wait_ge(scaled_done, tb + 1)
                nc.vector.tensor_scalar(xq[:, :, :], scaled[:, :, :], QB - FFN_EPS, FFN_EPS - QB,
                                        ALU.min, ALU.max).then_inc(xq_done, 1)

            def add(tb):
                if tb >= 2:
                    dve.wait_ge(y_sent[tb % 2], tb // 2 * 16)
                for k in range(TPB):
                    dve.wait_ge(y_ready, tb * 2 + k // 2 + 1)
                    nc.vector.scalar_tensor_tensor(out=y[:, tb % 2, k, :], in0=y_bank[k // 2][:, (k % 2) * E:(k % 2 + 1) * E],
                                                   scalar=back[:, :], in1=x[:, tb * TPB + k, :],
                                                   op0=ALU.mult, op1=ALU.add).then_inc(y_added, 1)

            clip(0)
            for tb in range(NB):
                if tb + 1 < NB:
                    clip(tb + 1)
                add(tb)

        @block.scalar
        def _(act):
            act.wait_ge(factor_done, 4)
            for tb in range(NB):
                act.wait_ge(xq_done, tb)
                nc.scalar.activation(scaled[:, :, :], x3[:, tb * TPB:(tb + 1) * TPB, :], ACT.Copy,
                                     scale=to_q[:, :]).then_inc(scaled_done, 1)
                act.wait_ge(y_ready, tb * 2)
                for c in range(EC):
                    act.wait_ge(xt_ready, tb * EC + c + 1)
                    nc.scalar.activation(xq_t[:, c, :], x_bank[c], ACT.Copy).then_inc(xt_copied, 1)

        @block.tensor
        def _(pe):
            for tb in range(NB):
                pe.wait_ge(xq_done, tb + 1)
                pe.wait_ge(xt_copied, tb * EC)
                for c in range(EC):
                    for k in range(TPB):
                        last = nc.tensor.transpose(x_bank[c][:, k * P:(k + 1) * P], xq[:, k, c * P:(c + 1) * P],
                                                   ident[:, :])
                    last.then_inc(xt_ready, 1)
                pe.wait_ge(xt_copied, tb * EC + EC)
                pe.wait_ge(y_added, tb * TPB)
                for k in range(TPB):
                    for c in range(EC):
                        last = nc.tensor.matmul(y_bank[k // 2][:, (k % 2) * E:(k % 2 + 1) * E],
                                                xq_t[:, c, k * P:(k + 1) * P], w_tern[:, c, :],
                                                start=c == 0, stop=c == EC - 1)
                    if k % 2:
                        last.then_inc(y_ready, 1)

def build(nc, io):
    with ExitStack() as outer:
        def sb(name, shape, dt=F32):
            return outer.enter_context(nc.sbuf_tensor(name, shape, dt))

        psum = outer.enter_context(nc.psum_tensor("psum", [P, 8 * BLK], F32))
        keep = {"x": sb("x_sb", [P, TILES, E]), "ident": sb("ident", [P, P])}
        with ExitStack() as own:
            def sbo(name, shape, dt=F32):
                return own.enter_context(nc.sbuf_tensor(name, shape, dt))

            keep["attn"] = sbo("attn", [P, TILES, E])
            with ExitStack() as early:
                def sbe(name, shape, dt=F32):
                    return early.enter_context(nc.sbuf_tensor(name, shape, dt))

                keep["v_all"] = sbe("v_all", [P, TILES, H, VW])
                keep["mask_row"] = sbe("mask_row", [P, P + PAGE], BF16)
                keep["ones"] = sbe("ones", [P, PAGE], BF16)
                with ExitStack() as ctx:
                    project(nc, ctx, io, keep, psum)
                with ExitStack() as ctx:
                    attend(nc, ctx, io, keep, psum)
            keep["x2_t"] = sbo("x2_t", [P, EC, NB, BLK])
            keep["row_fill"] = sbo("row_fill", [P, TILES])
            keep["ctx_t"] = sbo("ctx_t", [P, EC, S2])
            keep["w_qk"] = sbo("w_qk", [P, EC, E])
            keep["bias_c"] = sbo("bias_c", [P, EC])
            keep["v_out"] = sbo("v_out", [P, S2_TILES, E])
            keep["w_tern"] = sbo("w_tern", [P, EC, E])
            keep["beta"] = sbo("beta", [P, 1])
            keep["abs_max"] = sbo("abs_max", [P, TILES])
            with ExitStack() as ctx:
                fold(nc, ctx, io, keep, psum)
            keep["x3"] = keep["attn"]
            with ExitStack() as ctx:
                cross(nc, ctx, io, keep, psum)
            with ExitStack() as ctx:
                feed(nc, ctx, io, keep, psum)

def rope_tables():
    import numpy as np

    inv = 1.0 / 10000.0 ** (np.arange(0, D, 2, dtype=np.float32) / D)
    ang = np.outer(np.arange(T, dtype=np.float32), inv)
    return (np.ascontiguousarray(np.cos(ang).astype(np.float32).T),
            np.ascontiguousarray(np.sin(ang).astype(np.float32).T))

def kernel(x, ctx_1024, mask_BxSxS2_ik1, L0_attn_wq, L0_attn_w_down, L0_attn_wk_up, L0_attn_wv_up, L0_attn_wo,
           L0_xattn_Wq, L0_xattn_bq, L0_xattn_Wk, L0_xattn_bk, L0_xattn_Wv, L0_xattn_bv, L0_xattn_Wo, L0_xattn_bo,
           L0_ffn_weight, L0_ffn_ln_gamma, L0_ffn_ln_beta):
    import numpy as np
    import concourse.bacc as bacc
    from concourse.bass_utils import run_bass_kernel_spmd

    cos, sin = rope_tables()
    arrays = {
        "x": np.asarray(x)[0], "wq": L0_attn_wq, "w_down": L0_attn_w_down, "wk_up": L0_attn_wk_up,
        "wv_up": L0_attn_wv_up, "wo": L0_attn_wo, "cos": cos, "sin": sin,
        "ctxT": np.asarray(ctx_1024)[0].T, "mask": np.asarray(mask_BxSxS2_ik1)[0],
        "Wq": L0_xattn_Wq, "Wk": L0_xattn_Wk, "Wv": L0_xattn_Wv, "WoT": np.asarray(L0_xattn_Wo).T,
        "bq": L0_xattn_bq, "bk": L0_xattn_bk, "bv": L0_xattn_bv, "bo": L0_xattn_bo,
        "ffn_w": L0_ffn_weight, "gamma": L0_ffn_ln_gamma, "beta": L0_ffn_ln_beta,
    }
    arrays = {name: np.ascontiguousarray(a) for name, a in arrays.items()}
    nc = bacc.Bacc("TRN2", target_bir_lowering=False, num_devices=1)
    io = {name: nc.dram_tensor("in_" + name, a.shape, mybir.dt.from_np(a.dtype), kind="ExternalInput").ap()
          for name, a in arrays.items()}
    io["pieces"] = nc.dram_tensor("pieces", (2, NB, 3, 2, HALF, H, BLK), BF16, kind="Internal").ap()
    io["out"] = nc.dram_tensor("out", (T, E), F32, kind="ExternalOutput").ap()
    build(nc, io)
    got = run_bass_kernel_spmd(nc, [{"in_" + name: a for name, a in arrays.items()}], core_ids=[0])
    return got.results[0]["out"].reshape(1, T, E)
```
